# Optimizing a Trainium2 kernel written in Bass

```python
import numpy as np
import jax
import jax.numpy as jnp

def _softmax(x, axis=-1):
    return jax.nn.softmax(x, axis=axis)

def _gelu(x):
    return jax.nn.gelu(x, approximate=True)

def _silu(x):
    return jax.nn.silu(x)

def _sigmoid(x):
    return jax.nn.sigmoid(x)

def _layernorm(x, axis=-1, eps=1e-05):
    m = jnp.mean(x, axis=axis, keepdims=True)
    v = jnp.var(x, axis=axis, keepdims=True)
    return (x - m) / jnp.sqrt(v + eps)

def _scatter_add(tgt, idx, src, axis=0):
    return tgt.at[idx].add(src)

def _segment_sum(src, seg, n):
    return jax.ops.segment_sum(src, seg, n)
kernel_name = 'mk_seq_postln_d1_jaxref_r4_6f3937'

def setup_inputs(seed: int=0):
    np.random.seed(seed)
    _w = jnp.asarray

    def _L0_attn_setup():
        import jax, jax.numpy as jnp
        import numpy as np
        D_MODEL = 256
        N_HEADS = 16
        D_HIDDEN = 1024
        BATCH = 2
        N_CTX = 512

        def _split_heads(t, n_heads):
            B, S, D = t.shape
            return t.reshape(B, S, n_heads, D // n_heads).transpose(0, 2, 1, 3)
        key = jax.random.key(seed)
        ks = jax.random.split(key, 4)
        scale = 0.02
        x = jax.random.normal(ks[0], (BATCH, N_CTX, D_MODEL), dtype=jnp.float32)
        Wk = jax.random.normal(ks[1], (D_MODEL, D_MODEL), dtype=jnp.float32) * scale
        bk = jnp.zeros((D_MODEL,), dtype=jnp.float32)
        Wv = jax.random.normal(ks[2], (D_MODEL, D_HIDDEN), dtype=jnp.float32) * scale
        bv = jnp.zeros((D_HIDDEN,), dtype=jnp.float32)
        Wf = jax.random.normal(ks[3], (D_HIDDEN, D_MODEL), dtype=jnp.float32) * scale
        bf = jnp.zeros((D_MODEL,), dtype=jnp.float32)
        return {'x': x, 'Wk': Wk, 'bk': bk, 'Wv': Wv, 'bv': bv, 'Wf': Wf, 'bf': bf}
    _L0_attn_in = _L0_attn_setup()

    def _L0_ffn_setup():
        import jax, jax.numpy as jnp
        import numpy as np
        DIM = 256
        HIDDEN = 768
        SCALE = 1.0 / 127.0

        def _dequant(w_int, dtype):
            return w_int.astype(dtype) * jnp.asarray(SCALE, dtype)
        key = jax.random.key(seed)
        k_x, k_g, k_u, k_d = jax.random.split(key, 4)
        x = jax.random.normal(k_x, (4, 512, DIM), dtype=jnp.float32)
        w_gate = jax.random.randint(k_g, (HIDDEN, DIM), -127, 128, dtype=jnp.int32)
        w_up = jax.random.randint(k_u, (HIDDEN, DIM), -127, 128, dtype=jnp.int32)
        w_down = jax.random.randint(k_d, (DIM, HIDDEN), -127, 128, dtype=jnp.int32)
        return {'x': x, 'w_gate': w_gate, 'w_up': w_up, 'w_down': w_down}
    _L0_ffn_in = _L0_ffn_setup()
    _d = {'L0_attn_x': _L0_attn_in['x'], 'L0_attn_Wk': _L0_attn_in['Wk'], 'L0_attn_bk': _L0_attn_in['bk'], 'L0_attn_Wv': _L0_attn_in['Wv'], 'L0_attn_bv': _L0_attn_in['bv'], 'L0_attn_Wf': _L0_attn_in['Wf'], 'L0_attn_bf': _L0_attn_in['bf'], 'L0_ffn_w_gate': _L0_ffn_in['w_gate'], 'L0_ffn_w_up': _L0_ffn_in['w_up'], 'L0_ffn_w_down': _L0_ffn_in['w_down']}
    _x0 = _d['L0_attn_x']
    _d['L0_attn_x'] = jax.random.normal(jax.random.fold_in(jax.random.key(seed), 1), (8, 1024, 256), dtype=_x0.dtype)
    del _x0
    return _d

def reference(L0_attn_x, L0_attn_Wk, L0_attn_bk, L0_attn_Wv, L0_attn_bv, L0_attn_Wf, L0_attn_bf, L0_ffn_w_gate, L0_ffn_w_up, L0_ffn_w_down):

    def _L0_attn_ref(x, Wk, bk, Wv, bv, Wf, bf):
        import jax, jax.numpy as jnp
        import numpy as np
        D_MODEL = 256
        N_HEADS = 16
        D_HIDDEN = 1024
        BATCH = 2
        N_CTX = 512

        def _split_heads(t, n_heads):
            B, S, D = t.shape
            return t.reshape(B, S, n_heads, D // n_heads).transpose(0, 2, 1, 3)
        B, S, D = x.shape
        H = N_HEADS
        Q = _split_heads(x, H)
        K = _split_heads(x @ Wk + bk, H)
        V = _split_heads(x @ Wv + bv, H)
        causal = jnp.tril(jnp.ones((S, S), dtype=bool))
        mask = jnp.where(causal, 0.0, -jnp.inf).astype(x.dtype)
        scores = jnp.einsum('bhqd,bhkd->bhqk', Q, K) + mask
        attn = jax.nn.softmax(scores, axis=-1)
        o = jnp.einsum('bhqk,bhkd->bhqd', attn, V)
        o = o.transpose(0, 2, 1, 3).reshape(B, S, -1)
        return x + jax.nn.gelu(o, approximate=False) @ Wf + bf

    def _L0_ffn_ref(x, w_gate, w_up, w_down):
        import jax, jax.numpy as jnp
        import numpy as np
        DIM = 256
        HIDDEN = 768
        SCALE = 1.0 / 127.0

        def _dequant(w_int, dtype):
            return w_int.astype(dtype) * jnp.asarray(SCALE, dtype)
        wg = _dequant(w_gate, x.dtype)
        wu = _dequant(w_up, x.dtype)
        wd = _dequant(w_down, x.dtype)
        gate = jnp.einsum('bsd,hd->bsh', x, wg)
        up = jnp.einsum('bsd,hd->bsh', x, wu)
        h = jax.nn.silu(gate) * up
        return jnp.einsum('bsh,dh->bsd', h, wd)
    x = L0_attn_x
    x = _layernorm(x + _L0_attn_ref(x, L0_attn_Wk, L0_attn_bk, L0_attn_Wv, L0_attn_bv, L0_attn_Wf, L0_attn_bf), axis=-1)
    x = _layernorm(x + _L0_ffn_ref(x, L0_ffn_w_gate, L0_ffn_w_up, L0_ffn_w_down), axis=-1)
    return x

_drawn_inputs = setup_inputs


def setup_inputs(seed=0):
    import zlib

    import numpy as np

    out = dict(_drawn_inputs(seed))
    spreads = {'L0_attn_bk': (0.0, 0.8), 'L0_attn_bv': (0.0, 0.372), 'L0_attn_bf': (0.0, 0.1)}
    factors = {'L0_attn_Wk': 5.078, 'L0_attn_Wv': 4.415}
    for name, (base, spread) in spreads.items():
        noise = np.random.default_rng([zlib.crc32(name.encode()), seed]).standard_normal(out[name].shape)
        drawn = base * np.exp(spread * noise) if base else spread * noise
        out[name] = jnp.asarray(drawn.astype(out[name].dtype))
    for name, factor in factors.items():
        out[name] = (out[name] * factor).astype(out[name].dtype)
    return out
```

```python
from contextlib import ExitStack

import concourse.bass as bass
from concourse import mybir

F32 = mybir.dt.float32
F32R = mybir.dt.float32r
BF16 = mybir.dt.bfloat16
I32 = mybir.dt.int32
ALU = mybir.AluOpType
ACT = mybir.ActivationFunctionType
AX = mybir.AxisListType

P = 128
BANK = 512
PARTS = 3
Q_ROWS = (0, 0, 1, 1, 0, 2)
K_ROWS = (0, 1, 0, 1, 2, 0)
MASKED = -1.0e30
EPS = 1.0e-5
LN_EXP = "natural_log_exp_and_others"
QSCALE = 1.0 / 127.0


def walk(eng, steps, first, unroll, rounds, body):
    for r in range(first):
        body(r, 0)
    with eng.Fori(0, rounds) as it:
        for k in range(unroll):
            body(first + k, it)
    for r in range(first + unroll * rounds, steps):
        body(r, 0)


def settle(eng, passed):
    eng.sem_inc(passed, 1)


def build(nc, xT, x, Wk, bk, Wv, bv, Wf, bf, wg, wu, wd, out):
    B, D, S = xT.shape
    HV = Wv.shape[1]
    FH = wg.shape[1]
    DH = 16
    H = D // DH
    DV = HV // H
    DC = D // P
    HC = HV // P
    FC = FH // P
    NT = S // P
    PAIRS = B * H // 2
    SPL = len(Q_ROWS) * DH
    ROWS = SPL + PARTS
    U = BANK
    UT = U // P
    UNITS = B * S // U
    assert DH * 8 == P and DV * 2 == P and S == 2 * U and SPL == 96 and UT == 4

    qd = nc.dram_tensor("q_parts", (PARTS, B * D, S), BF16, kind="Internal").ap()
    kd = nc.dram_tensor("k_parts", (PARTS, B * D, S), BF16, kind="Internal").ap()
    vd = nc.dram_tensor("v_pairs", (PAIRS, NT, P, P), F32, kind="Internal").ap()
    od = nc.dram_tensor("o_heads", (B, HV, S), F32, kind="Internal").ap()
    sd = nc.dram_tensor("shifts", (PAIRS, PARTS * 2 * NT, P), BF16, kind="Internal").ap()

    with ExitStack() as ctx:
        def sb(name, shape, dt, c=ctx):
            return c.enter_context(nc.sbuf_tensor(name, shape, dt))

        def sem(name):
            return ctx.enter_context(nc.semaphore(name))

        ident16 = sb("ident16", [P, P], BF16)
        ident32 = sb("ident32", [P, P], F32)
        causal = sb("causal", [P, P], BF16)
        bk_sb = sb("bk_sb", [P, DC], F32)
        bv_sb = sb("bv_sb", [P, HC], F32)
        bf_sb = sb("bf_sb", [P, D], F32)
        eps_sb = sb("eps_sb", [P, 1], F32)
        wk_hi = sb("wk_hi", [P, DC, D], F32R)
        wk_lo = sb("wk_lo", [P, DC, D], F32R)
        wv_hi = sb("wv_hi", [P, DC, HV], F32R)
        wv_lo = sb("wv_lo", [P, DC, HV], F32R)
        wf_sb = sb("wf_sb", [P, HC, D], F32)
        wg_sb = sb("wg_sb", [P, DC, FH], F32R)
        wu_sb = sb("wu_sb", [P, DC, FH], F32R)
        wd_sb = sb("wd_sb", [P, FC, D], F32)

        RING = 4
        Q = [sb(f"q_stack{i}", [ROWS, 2, S], BF16) for i in range(RING)]
        K = [sb(f"k_stack{i}", [ROWS, 2, S], BF16) for i in range(RING)]
        V = [sb(f"v_pair{i}", [P, NT, P], F32) for i in range(RING)]
        negmax = [sb(f"negmax{i}", [P, 2 * NT], F32) for i in range(2)]
        den = [sb(f"den{i}", [P, 2 * NT], F32) for i in range(2)]
        lnden = sb("lnden", [P, 2 * NT], F32)
        shift = sb("shift", [P, 2 * NT], F32)
        shift_r1 = sb("shift_r1", [P, 2 * NT], F32)
        shift_r2 = sb("shift_r2", [P, 2 * NT], F32)
        shift_parts = sb("shift_parts", [P, PARTS, 2 * NT], BF16)
        shiftT = sb("shiftT", [PARTS * 2 * NT, P], BF16)
        bctx = ExitStack()
        W = [[sb(f"weights{h}{i}", [P, S], F32, bctx) for i in range(2)] for h in range(2)]
        scrap = [sb(f"scrap{h}", [P, S], BF16, bctx) for h in range(2)]
        osb = [sb(f"o_pair{i}", [P, S], F32, bctx) for i in range(2)]
        bctx.close()

        actx = ExitStack()
        wk_in = sb("wk_in", [P, DC, D], F32, actx)
        wv_in = sb("wv_in", [P, DC, HV], F32, actx)
        wi_in = [sb(f"wi_in{i}", [P, DC * FH], I32, actx) for i in range(3)]
        actx.close()
        actx = ExitStack()
        xt = [sb(f"xt{i}", [P, DC, U], F32, actx) for i in range(2)]
        x_hi = [sb(f"x_hi{i}", [P, DC, U], F32R, actx) for i in range(2)]
        x_lo = [sb(f"x_lo{i}", [P, DC, U], F32R, actx) for i in range(2)]
        q_r1 = sb("q_r1", [P, DC, U], F32, actx)
        qp = [sb(f"q_split{i}", [P, PARTS, DC, U], BF16, actx) for i in range(2)]
        kf = sb("kf", [P, DC, U], F32, actx)
        k_r1 = sb("k_r1", [P, DC, U], F32, actx)
        kp = [sb(f"k_split{i}", [P, PARTS, DC, U], BF16, actx) for i in range(2)]
        vs = [sb(f"v_unit{i}", [P, UT, HV], F32, actx) for i in range(2)]
        actx.close()
        g = [sb(f"g{i}", [P, HC, U], F32) for i in range(2)]
        xn = [sb(f"xn{i}", [P, UT, D], F32) for i in range(2)]
        y_pre = sb("y_pre", [P, UT, D], F32)
        y = [sb(f"y{i}", [P, UT, D], F32) for i in range(2)]
        y_hi = sb("y_hi", [P, DC, U], F32R)
        y_lo = sb("y_lo", [P, DC, U], F32R)
        sg = [sb(f"silu_gate{i}", [P, U], F32) for i in range(2)]
        hT = sb("hT", [P, FC, U], F32)
        z_pre = sb("z_pre", [P, UT, D], F32)
        z = [sb(f"z{i}", [P, UT, D], F32) for i in range(2)]
        stats = sb("stats", [P, 2 * UT, nc.vector.BN_STATS_DIM], F32)
        mv = sb("mean_var", [P, 2 * UT, 2], F32)
        lnvar = sb("lnvar", [P, 2 * UT], F32)
        rstd0 = sb("rstd0", [P, 2 * UT], F32)
        newt = sb("newton", [P, 3, 2 * UT], F32)
        rstd = sb("rstd", [P, 2 * UT], F32)

        sc = [ctx.enter_context(nc.psum_tensor(f"scores{h}", [P, 2 * BANK], F32)) for h in range(2)]
        st = [ctx.enter_context(nc.psum_tensor(f"scoresT{i}", [P, BANK], F32)) for i in range(2)]
        oo = ctx.enter_context(nc.psum_tensor("o_acc", [P, 2 * BANK], F32))
        a_banks = [sc[0][:, 0:BANK], sc[0][:, BANK:], sc[1][:, 0:BANK], sc[1][:, BANK:], st[0][:, :]]
        shiftT_ps = sc[0][:, BANK:].bitcast(BF16)[0:PARTS * 2 * NT, 0:P]

        s_wkv_in = sem("wkv_loaded")
        s_w_in = sem("other_weights_loaded")
        s_blank = sem("constants_blanked")
        s_const = sem("constants_ready")
        s_w_hi = sem("weights_hi_ready")
        s_wkv = sem("wkv_split")
        s_wrest = sem("ffn_weights_ready")
        s_passed = {e: sem(f"passed_{e}") for e in ("sp", "pool", "pe", "dve")}
        s_xt = [sem(f"xt_loaded{i}") for i in range(2)]
        s_xhi = sem("x_hi_ready")
        s_xs = sem("x_split")
        s_q1 = sem("q_part1_ready")
        s_qr = sem("q_rest_ready")
        s_q2 = sem("q_part2_ready")
        s_q3 = sem("q_part3_ready")
        s_job = sem("projection_ready")
        s_eva = sem("projection_copied_by_act")
        s_evd = sem("projection_copied_by_dve")
        s_k1 = sem("k_part1_ready")
        s_kr = sem("k_rest_ready")
        s_k2 = sem("k_part2_ready")
        s_k3 = sem("k_part3_ready")
        s_qst = [sem(f"q_stored{i}") for i in range(2)]
        s_kst = [sem(f"k_stored{i}") for i in range(2)]
        s_vst = [sem(f"v_stored{i}") for i in range(2)]
        s_stack = [sem(f"stack_loaded{i}") for i in range(RING)]
        s_sc = sem("scores_ready")
        s_max = sem("negmax_ready")
        s_den = sem("den_ready")
        s_ln = sem("lnden_ready")
        s_shc = sem("shift_chain")
        s_shp = sem("shift_parts_ready")
        s_sht = sem("shiftT_ready")
        s_shs = sem("shiftT_copied")
        s_shd = sem("shift_in_dram")
        s_shl = [sem(f"shift_rows_loaded{i}") for i in range(RING)]
        s_st = sem("scoresT_ready")
        s_w = sem("weights_made")
        s_sel = sem("weights_masked")
        s_pv = sem("weights_used")
        s_oev = sem("o_copied")
        s_ost = [sem(f"o_stored{i}") for i in range(2)]
        s_g = [sem(f"g_loaded{i}") for i in range(2)]
        s_xn = [sem(f"xn_loaded{i}") for i in range(2)]
        s_gelu = sem("gelu_done")
        s_wf = sem("wf_ready")
        s_x2 = sem("x_doubled")
        s_y = sem("y_pre_ready")
        s_bs = sem("stats_ready")
        s_mv = sem("mean_var_ready")
        s_lv = sem("lnvar_ready")
        s_r0 = sem("rstd0_ready")
        s_nw = sem("newton_chain")
        s_yn = sem("y_ready")
        s_zn = sem("z_ready")
        s_yt = sem("yT_ready")
        s_yh = sem("y_hi_ready")
        s_yl = sem("y_lo_ready")
        s_gu = sem("gate_up_ready")
        s_si = sem("silu_ready")
        s_h = sem("h_ready")
        s_dn = sem("down_ready")
        s_z = sem("z_pre_ready")
        s_out = [sem(f"out_stored{i}") for i in range(2)]

        block = ctx.enter_context(nc.Block())

        JOBS = [("k", c, 0) for c in range(DC)] + [("v", i, hf) for i in range(UT) for hf in range(2)]
        BY_ACT = [j for j in range(len(JOBS)) if j < DC or j % 2]
        BY_DVE = [j for j in range(len(JOBS)) if j not in BY_ACT]
        NB = len(a_banks)
        NJ = len(JOBS)

        def copied(j):
            if j in BY_ACT:
                return s_eva, len(BY_ACT), BY_ACT.index(j) + 1
            return s_evd, len(BY_DVE), BY_DVE.index(j) + 1

        def chunks(u):
            return [(P * u, BANK), (BANK, S)] if P * u < BANK else [(P * u, S)]

        CH = [len(chunks(u)) for u in range(NT)]
        PER_ST = 2 * sum(CH)

        def made(u, h):
            return 2 * sum(CH[:u]) + (CH[u] if h else 0)

        LOOP_A = (UNITS, 2, 2, (UNITS - 4) // 2)
        LAG = 2
        STEPS_B = PAIRS + LAG
        LOOP_B = (STEPS_B, 4, 4, (PAIRS - 8) // 4)
        STEPS_C = UNITS + 1
        LOOP_C = (STEPS_C, 3, 2, (UNITS - 6) // 2)

        def unit_of(r, it):
            return r // 2 + it, (r % 2) * U

        @block.sync
        def _(sp):
            sp.dma_start(wk_in[:], Wk.rearrange("(c p) n -> p c n", p=P)).then_inc(s_wkv_in, 16)
            sp.dma_start(wv_in[:], Wv.rearrange("(c p) n -> p c n", p=P)).then_inc(s_wkv_in, 16)
            sp.dma_start(bk_sb[:], bk).then_inc(s_w_in, 16)
            sp.dma_start(bv_sb[:], bv).then_inc(s_w_in, 16)
            sp.dma_start(bf_sb[:], bf.partition_broadcast(P)).then_inc(s_w_in, 16)
            sp.dma_start(wf_sb[:], Wf.rearrange("(c p) n -> p c n", p=P)).then_inc(s_w_in, 16)
            sp.dma_start(wi_in[0][:].rearrange("p (c n) -> p c n", c=DC),
                         wg.rearrange("(c p) n -> p c n", p=P)).then_inc(s_w_in, 16)
            sp.dma_start(wi_in[1][:].rearrange("p (c n) -> p c n", c=DC),
                         wu.rearrange("(c p) n -> p c n", p=P)).then_inc(s_w_in, 16)
            sp.dma_start(wi_in[2][:].rearrange("p (c n) -> p c n", c=FC),
                         wd.rearrange("(c p) n -> p c n", p=P)).then_inc(s_w_in, 16)
            sp.wait_ge(s_wkv, 2)
            sp.wait_ge(s_wrest, 3)

            def load_x(r, it):
                b, t0 = unit_of(r, it)
                if r >= 2:
                    sp.wait_ge(s_xs, r - 1 + 2 * it)
                    settle(sp, s_passed["sp"])
                    sp.wait_ge(s_qr, r - 1 + 2 * it)
                    settle(sp, s_passed["sp"])
                sp.dma_start(xt[r % 2][:], xT[bass.ds(b, 1), :, t0:t0 + U].rearrange(
                    "o (c p) t -> (o p) c t", p=P)).then_inc(s_xt[r % 2], 16)

            def project(r, it):
                n = r + 2 * it
                b, t0 = unit_of(r, it)
                if r < UNITS - 1:
                    load_x(r + 1, it)
                sp.wait_ge(s_q3, n + 1)
                settle(sp, s_passed["sp"])
                for m in range(PARTS):
                    sp.dma_start(qd[m, bass.ds(b * D, D), t0:t0 + U].rearrange("(c p) t -> p c t", p=P),
                                 qp[r % 2][:, m]).then_inc(s_qst[r % 2], 16)
                sp.wait_ge(s_k3, DC * (n + 1))
                settle(sp, s_passed["sp"])
                for m in range(PARTS):
                    sp.dma_start(kd[m, bass.ds(b * D, D), t0:t0 + U].rearrange("(c p) t -> p c t", p=P),
                                 kp[r % 2][:, m]).then_inc(s_kst[r % 2], 16)
                sp.wait_ge(s_eva, len(BY_ACT) * (n + 1))
                settle(sp, s_passed["sp"])
                sp.wait_ge(s_evd, len(BY_DVE) * (n + 1))
                settle(sp, s_passed["sp"])
                for i in range(UT):
                    sp.dma_start(vd[bass.ds(b * HC, HC), t0 // P + i].rearrange("h t v -> t h v"),
                                 vs[r % 2][:, i].rearrange("t (h v) -> t h v", v=P)
                                 ).then_inc(s_vst[r % 2], 16)

            load_x(0, 0)
            walk(sp, *LOOP_A, project)
            for i in range(2):
                sp.wait_ge(s_qst[i], 16 * PARTS * UNITS // 2)
                sp.wait_ge(s_kst[i], 16 * PARTS * UNITS // 2)
                sp.wait_ge(s_vst[i], 16 * UT * UNITS // 2)

            def load_pair(r, it):
                n = r + RING * it
                slot = r % RING
                if r >= RING:
                    sp.wait_ge(s_pv, NT * (n - RING + 1))
                    settle(sp, s_passed["sp"])
                for (stack, parts, rows) in ((Q, qd, Q_ROWS), (K, kd, K_ROWS)):
                    for i, m in enumerate(rows):
                        sp.dma_start(stack[slot][DH * i:DH * (i + 1), :, :],
                                     parts[m, bass.ds(n * 2 * DH, 2 * DH), :].rearrange(
                                         "(h d) t -> d h t", d=DH)).then_inc(s_stack[slot], 16)
                sp.dma_start(V[slot][:], vd[bass.ds(n, 1)].rearrange("o k t v -> (o t) k v")
                             ).then_inc(s_stack[slot], 16)

            def attend(r, it):
                n = r + RING * it
                if r + 1 < PAIRS:
                    load_pair(r + 1, it)
                if 1 <= r <= PAIRS:
                    sp.wait_ge(s_shs, n)
                    settle(sp, s_passed["sp"])
                    sp.dma_start(sd[bass.ds(n - 1, 1)].rearrange("o a t -> (o a) t"),
                                 shiftT[:]).then_inc(s_shd, 16)
                    sp.wait_ge(s_shd, 16 * n)
                    settle(sp, s_passed["sp"])
                    slot = (r - 1) % RING
                    sp.dma_start(Q[slot][SPL:ROWS, :, :].rearrange("m h t -> m (h t)"),
                                 sd[bass.ds(n - 1, 1)].rearrange("o (m a) t -> (o m) (a t)", m=PARTS)
                                 ).then_inc(s_shl[slot], 16)
                if r >= LAG + 1:
                    sp.wait_ge(s_oev, n - LAG)
                    settle(sp, s_passed["sp"])
                    store_o(r - LAG - 1, n - LAG - 1)

            def store_o(r, n):
                sp.dma_start(od.rearrange("b h t -> (b h) t")[bass.ds(n * P, P), :],
                             osb[r % 2][:]).then_inc(s_ost[r % 2], 16)

            load_pair(0, 0)
            walk(sp, *LOOP_B, attend)
            sp.wait_ge(s_oev, PAIRS)
            store_o(PAIRS - 1, PAIRS - 1)
            for i in range(2):
                sp.wait_ge(s_ost[i], 16 * PAIRS // 2)

            def load_unit(r, it):
                b, t0 = unit_of(r, it)
                n = r + 2 * it
                if r >= 2:
                    sp.wait_ge(s_wf, UT * (n - 1))
                    settle(sp, s_passed["sp"])
                    sp.wait_ge(s_y, UT * (n - 1))
                    settle(sp, s_passed["sp"])
                sp.dma_start(g[r % 2][:], od[bass.ds(b, 1), :, t0:t0 + U].rearrange(
                    "o (c p) t -> (o p) c t", p=P)).then_inc(s_g[r % 2], 16)
                sp.dma_start(xn[r % 2][:], x[bass.ds(n * U, U), :].rearrange(
                    "(i p) d -> p i d", p=P)).then_inc(s_xn[r % 2], 16)

            def finish(r, it):
                n = r + 2 * it
                if r + 2 < UNITS:
                    load_unit(r + 2, it)
                if r >= 1:
                    sp.wait_ge(s_zn, UT * n)
                    settle(sp, s_passed["sp"])
                    sp.dma_start(out[bass.ds((n - 1) * U, U), :].rearrange("(i p) d -> p i d", p=P),
                                 z[(r - 1) % 2][:]).then_inc(s_out[(r - 1) % 2], 16)

            load_unit(0, 0)
            load_unit(1, 0)
            walk(sp, *LOOP_C, finish)
            for i in range(2):
                sp.wait_ge(s_out[i], 16 * UNITS // 2)

        @block.gpsimd
        def _(pool):
            pool.memset(ident16[:], 0.0).then_inc(s_blank, 1)
            pool.memset(ident32[:], 0.0).then_inc(s_blank, 1)
            pool.memset(causal[:], 0.0).then_inc(s_blank, 1)
            pool.wait_ge(s_blank, 3)
            for m in (ident16, ident32):
                pool.affine_select(out=m[:], in_=m[:], compare_op=ALU.not_equal, fill=1.0, base=0,
                                   pattern=[[-1, P]], channel_multiplier=1).then_inc(s_const, 1)
            pool.affine_select(out=causal[:], in_=causal[:], compare_op=ALU.is_ge, fill=MASKED, base=0,
                               pattern=[[-1, P]], channel_multiplier=1).then_inc(s_const, 1)

            def project(r, it):
                n = r + 2 * it
                pool.wait_ge(s_q1, n + 1)
                if r > 0:
                    pool.wait_ge(s_q3, n)
                pool.tensor_tensor(q_r1[:], xt[r % 2][:], qp[r % 2][:, 0], ALU.subtract).then_inc(s_qr, 1)
                pool.wait_ge(s_q2, n + 1)
                pool.tensor_tensor(qp[r % 2][:, 2], q_r1[:], qp[r % 2][:, 1], ALU.subtract).then_inc(s_q3, 1)

            walk(pool, *LOOP_A, project)

            def attend(r, it):
                if r < LAG:
                    return
                n = r - LAG + RING * it
                for u in range(NT):
                    for h in range(2):
                        pool.wait_ge(s_w, PER_ST * n + made(u, h) + 1)
                        settle(pool, s_passed["pool"])
                        diag = W[h][u % 2][:, P * u:P * (u + 1)]
                        pool.affine_select(out=diag, in_=diag, compare_op=ALU.is_ge, fill=0.0, base=0,
                                           pattern=[[1, P]], channel_multiplier=-1).then_inc(s_sel, 1)

            walk(pool, *LOOP_B, attend)

        @block.tensor
        def _(pe):
            def mm(o, l, r, start, stop):
                return nc.tensor.matmul(o, l, r, start=start, stop=stop)

            pe.wait_ge(s_wkv, 2)

            def project(r, it):
                n = r + 2 * it
                hi, lo = x_hi[r % 2], x_lo[r % 2]
                pe.wait_ge(s_xs, n + 1)
                for j, (what, i, hf) in enumerate(JOBS):
                    s, per, at = copied((j - NB) % NJ)
                    if j >= NB:
                        pe.wait_ge(s, per * n + at)
                    elif r > 0:
                        pe.wait_ge(s, per * (n - 1) + at)
                    bank = a_banks[j % NB]
                    last = 3 * DC - 1
                    for c in range(DC):
                        if what == "k":
                            cols = slice(P * i, P * (i + 1))
                            terms = ((wk_hi[:, c, cols], hi[:, c]), (wk_hi[:, c, cols], lo[:, c]),
                                     (wk_lo[:, c, cols], hi[:, c]))
                        else:
                            toks, cols = slice(P * i, P * (i + 1)), slice(BANK * hf, BANK * (hf + 1))
                            terms = ((hi[:, c, toks], wv_hi[:, c, cols]), (hi[:, c, toks], wv_lo[:, c, cols]),
                                     (lo[:, c, toks], wv_hi[:, c, cols]))
                        for k, (l, m) in enumerate(terms):
                            e = mm(bank, l, m, 3 * c + k == 0, 3 * c + k == last)
                    e.then_inc(s_job, 1)

            walk(pe, *LOOP_A, project)
            pe.wait_ge(s_eva, len(BY_ACT) * UNITS)
            pe.wait_ge(s_evd, len(BY_DVE) * UNITS)
            pe.wait_ge(s_const, 3 + RING + 1)

            def score(h, u, r, n):
                q, k = Q[r % RING], K[r % RING]
                if u > 0 or r > 0:
                    pe.wait_ge(s_den, 2 * NT * n + 2 * u + h - 1)
                width = P * (u + 1)
                for c0 in range(0, width, BANK):
                    c1 = min(width, c0 + BANK)
                    mm(sc[h][:, c0:c1], q[0:SPL, h, P * u:P * (u + 1)], k[0:SPL, h, c0:c1], True, c1 < width)
                mm(sc[h][:, width - P:width], ident16[:], causal[:], False, True).then_inc(s_sc, 1)

            def scoreT(h, u, r, n):
                q, k = Q[r % RING], K[r % RING]
                for i, (c0, c1) in enumerate(chunks(u)):
                    c = made(u, h) + i
                    if r > 0 or c >= 2:
                        pe.wait_ge(s_w, PER_ST * n + c - 1)
                    mm(st[c % 2][:, 0:c1 - c0], k[:, h, P * u:P * (u + 1)], q[:, h, c0:c1],
                       True, True).then_inc(s_st, 1)

            def weigh(u, r, n):
                if u == 0 and r > 0:
                    pe.wait_ge(s_oev, n)
                pe.wait_ge(s_w, PER_ST * n + made(u + 1, 0))
                pe.wait_ge(s_sel, 2 * NT * n + 2 * (u + 1))
                for (c0, c1) in chunks(u):
                    for h in range(2):
                        e = mm(oo[DV * h:DV * (h + 1), c0:c1], V[r % RING][:, u, DV * h:DV * (h + 1)],
                               W[h][u % 2][:, c0:c1], u == 0, P * (u + 1) == c1)
                e.then_inc(s_pv, 1)

            def open_pair(r, it):
                pe.wait_ge(s_stack[r % RING], 16 * (len(Q_ROWS) + len(K_ROWS) + 1) * (r // RING + it + 1))

            def attend(r, it):
                n = r + RING * it
                weighing = r >= LAG
                m, rm = n - LAG, r - LAG
                if weighing:
                    pe.wait_ge(s_shl[rm % RING], 16 * (rm // RING + it + 1))
                    scoreT(0, 0, rm, m)
                for u in range(NT):
                    if u == 1 and 1 <= r <= PAIRS:
                        pe.wait_ge(s_shp, n)
                        settle(pe, s_passed["pe"])
                        nc.tensor.transpose(shiftT_ps, shift_parts[:].rearrange("p m a -> p (m a)"),
                                            ident16[:]).then_inc(s_sht, 1)
                    if u == 3 and 1 <= r < PAIRS:
                        pe.wait_ge(s_shs, n)

                    def next_score(h):
                        if u + 1 < NT and r < PAIRS:
                            score(h, u + 1, r, n)
                        elif u + 1 == NT and r + 1 < PAIRS:
                            if h == 0:
                                open_pair(r + 1, it)
                            score(h, 0, r + 1, n + 1)

                    next_score(0)
                    if weighing:
                        scoreT(1, u, rm, m)
                        if u > 0:
                            weigh(u - 1, rm, m)
                    next_score(1)
                    if weighing and u + 1 < NT:
                        scoreT(0, u + 1, rm, m)
                if weighing:
                    weigh(NT - 1, rm, m)

            open_pair(0, 0)
            score(0, 0, 0, 0)
            score(1, 0, 0, 0)
            walk(pe, *LOOP_B, attend)
            pe.wait_ge(s_oev, PAIRS)
            pe.wait_ge(s_wrest, 3)

            wf_ps, yt_ps, dn_ps = sc[0], sc[1], sc[1]
            gate_ps = [st[0][:, :], oo[:, 0:BANK]]
            up_ps = [st[1][:, :], oo[:, BANK:]]

            def wf_product(r, n):
                for i in range(UT):
                    if i == 0 and r > 0:
                        pe.wait_ge(s_y, UT * n)
                    for c in range(HC):
                        if i == 0:
                            pe.wait_ge(s_gelu, HC * n + c + 1)
                        e = mm(wf_ps[:, D * i:D * (i + 1)], g[r % 2][:, c, P * i:P * (i + 1)], wf_sb[:, c],
                               c == 0, c == HC - 1)
                    e.then_inc(s_wf, 1)

            def ffn(r, m):
                if r > 0:
                    pe.wait_ge(s_z, UT * m)
                for i in range(UT):
                    pe.wait_ge(s_yn, UT * m + i + 1)
                    for c in range(DC):
                        e = nc.tensor.transpose(yt_ps[:, BANK * c + P * i:BANK * c + P * (i + 1)],
                                                y[r % 2][:, i, P * c:P * (c + 1)], ident32[:])
                e.then_inc(s_yt, 1)
                pe.wait_ge(s_yl, DC * (m + 1))
                for f in range(FC):
                    if r > 0 or f >= 2:
                        pe.wait_ge(s_h, FC * m + f - 1)
                    cols = slice(P * f, P * (f + 1))
                    for ps, w in ((gate_ps[f % 2], wg_sb), (up_ps[f % 2], wu_sb)):
                        for c in range(DC):
                            for k, part in enumerate((y_hi, y_lo)):
                                e = mm(ps, w[:, c, cols], part[:, c], c + k == 0, c == DC - 1 and k == 1)
                    e.then_inc(s_gu, 1)
                for i in range(UT):
                    for f in range(FC):
                        if i == 0:
                            pe.wait_ge(s_h, FC * m + f + 1)
                        e = mm(dn_ps[:, D * i:D * (i + 1)], hT[:, f, P * i:P * (i + 1)], wd_sb[:, f],
                               f == 0, f == FC - 1)
                    e.then_inc(s_dn, 1)

            def finish(r, it):
                n = r + 2 * it
                if r < UNITS:
                    wf_product(r, n)
                if r >= 1:
                    ffn(r - 1, n - 1)

            walk(pe, *LOOP_C, finish)

        @block.scalar
        def _(act):
            def copy(o, i):
                return nc.scalar.activation(o, i, ACT.Copy)

            act.wait_ge(s_w_in, 16 * 7)

            def evacuate(j, r, n):
                what, i, hf = JOBS[j]
                act.wait_ge(s_job, NJ * n + j + 1)
                bank = a_banks[j % NB]
                if what == "k":
                    if r > 0:
                        act.wait_ge(s_kr, DC * (n - 1) + i + 1)
                    nc.scalar.activation(kf[:, i], bank, ACT.Identity, bias=bk_sb[:, i:i + 1]).then_inc(s_eva, 1)
                else:
                    copy(vs[r % 2][:, i, BANK * hf:BANK * (hf + 1)], bank).then_inc(s_eva, 1)

            def project(r, it):
                n = r + 2 * it
                par = r % 2
                stored = r // 2 + it
                act.wait_ge(s_xt[par], 16 * (stored + 1))
                if r >= 2:
                    act.wait_ge(s_qst[par], 16 * PARTS * stored)
                copy(qp[par][:, 0], xt[par][:]).then_inc(s_q1, 1)
                for c in range(DC):
                    evacuate(c, r, n)
                if r >= 2:
                    act.wait_ge(s_kst[par], 16 * PARTS * stored)
                for c in range(DC):
                    act.wait_ge(s_eva, len(BY_ACT) * n + c + 1)
                    copy(kp[par][:, 0, c], kf[:, c]).then_inc(s_k1, 1)
                act.wait_ge(s_qr, n + 1)
                copy(qp[par][:, 1], q_r1[:]).then_inc(s_q2, 1)
                if r >= 2:
                    act.wait_ge(s_vst[par], 16 * UT * stored)
                for k, j in enumerate(BY_ACT[DC:]):
                    if 1 <= k <= DC:
                        act.wait_ge(s_kr, DC * n + k)
                        copy(kp[par][:, 1, k - 1], k_r1[:, k - 1]).then_inc(s_k2, 1)
                    evacuate(j, r, n)

            walk(act, *LOOP_A, project)
            act.preload_act_table_set(LN_EXP)
            act.wait_ge(s_const, 3 + RING + 1)

            def attend(r, it):
                n = r + RING * it
                if 1 <= r <= PAIRS:
                    act.wait_ge(s_den, 2 * NT * n)
                    if r >= 2:
                        act.wait_ge(s_shp, n - 1)
                    nc.scalar.activation(lnden[:], den[(r - 1) % 2][:], ACT.Ln).then_inc(s_ln, 1)
                if r >= 2 and r < PAIRS:
                    act.wait_ge(s_shp, n - 1)
                for u in range(NT):
                    for h in range(2):
                        if r < PAIRS:
                            a = 2 * u + h
                            act.wait_ge(s_max, 2 * NT * n + a + 1)
                            width = P * (u + 1)
                            nc.scalar.activation(scrap[h][:, 0:width], sc[h][:, 0:width], ACT.Exp,
                                                 bias=negmax[r % 2][:, NT * h + u:NT * h + u + 1],
                                                 accum_out=den[r % 2][:, NT * h + u:NT * h + u + 1]
                                                 ).then_inc(s_den, 1)
                        if r >= LAG:
                            m, rm = n - LAG, r - LAG
                            for i, (c0, c1) in enumerate(chunks(u)):
                                c = made(u, h) + i
                                act.wait_ge(s_st, PER_ST * m + c + 1)
                                if i == 0 and (rm > 0 or u >= 2):
                                    act.wait_ge(s_pv, NT * m + u - 1)
                                nc.scalar.activation(W[h][u % 2][:, c0:c1], st[c % 2][:, 0:c1 - c0],
                                                     ACT.Exp).then_inc(s_w, 1)

            walk(act, *LOOP_B, attend)

            def gelus(r, n, stored):
                act.wait_ge(s_g[r % 2], 16 * (stored + 1))
                for c in range(HC):
                    nc.scalar.activation(g[r % 2][:, c], g[r % 2][:, c], ACT.Gelu,
                                         bias=bv_sb[:, c:c + 1]).then_inc(s_gelu, 1)

            gate_ps = [st[0][:, :], oo[:, 0:BANK]]
            gelus(0, 0, 0)

            def finish(r, it):
                n = r + 2 * it
                if r >= 1:
                    m = n - 1
                    act.wait_ge(s_yt, m + 1)
                    for c in range(DC):
                        copy(y_hi[:, c], sc[1][:, BANK * c:BANK * (c + 1)]).then_inc(s_yh, 1)
                    for f in range(FC):
                        act.wait_ge(s_gu, FC * m + f + 1)
                        nc.scalar.activation(sg[f % 2][:], gate_ps[f % 2], ACT.Silu,
                                             scale=QSCALE).then_inc(s_si, 1)
                a0, a1 = (0 if r < UNITS else UT), (2 * UT if r >= 1 else UT)
                act.preload_act_table_set(LN_EXP)
                act.wait_ge(s_mv, n + 1)
                nc.scalar.activation(lnvar[:, a0:a1], mv[:, a0:a1, 1], ACT.Ln, bias=eps_sb[:]).then_inc(s_lv, 1)
                act.wait_ge(s_lv, n + 1)
                nc.scalar.activation(rstd0[:, a0:a1], lnvar[:, a0:a1], ACT.Exp, scale=-0.5).then_inc(s_r0, 1)
                if r + 1 < UNITS:
                    gelus(r + 1, n + 1, (r + 1) // 2 + it)

            walk(act, *LOOP_C, finish)

        @block.vector
        def _(dve):
            v = nc.vector
            for i in range(RING):
                v.memset(K[i][SPL:ROWS, :, :], 1.0).then_inc(s_const, 1)
            v.memset(eps_sb[:], EPS).then_inc(s_const, 1)

            dve.wait_ge(s_wkv_in, 32)
            v.tensor_copy(wk_hi[:], wk_in[:]).then_inc(s_w_hi, 1)
            v.tensor_copy(wv_hi[:], wv_in[:]).then_inc(s_w_hi, 1)
            dve.wait_ge(s_w_hi, 2)
            v.tensor_tensor(wk_lo[:], wk_in[:], wk_hi[:].bitcast(F32), ALU.subtract).then_inc(s_wkv, 1)
            v.tensor_tensor(wv_lo[:], wv_in[:], wv_hi[:].bitcast(F32), ALU.subtract).then_inc(s_wkv, 1)
            dve.wait_ge(s_w_in, 16 * 7)
            for dst, src in ((wg_sb, wi_in[0]), (wu_sb, wi_in[1]), (wd_sb, wi_in[2])):
                v.tensor_copy(dst[:].rearrange("p c n -> p (c n)"), src[:]).then_inc(s_wrest, 1)

            def split_x(r, it):
                n = r + 2 * it
                dve.wait_ge(s_xt[r % 2], 16 * (r // 2 + it + 1))
                if r >= 2:
                    dve.wait_ge(s_job, NJ * (n - 1))
                v.tensor_copy(x_hi[r % 2][:], xt[r % 2][:]).then_inc(s_xhi, 1)
                dve.wait_ge(s_xhi, n + 1)
                v.tensor_tensor(x_lo[r % 2][:], xt[r % 2][:], x_hi[r % 2][:].bitcast(F32),
                                ALU.subtract).then_inc(s_xs, 1)

            def project(r, it):
                n = r + 2 * it
                par = r % 2
                if r >= 2:
                    dve.wait_ge(s_vst[par], 16 * UT * (r // 2 + it))
                for k, j in enumerate(BY_DVE):
                    what, i, hf = JOBS[j]
                    dve.wait_ge(s_job, NJ * n + j + 1)
                    v.tensor_copy(vs[par][:, i, BANK * hf:BANK * (hf + 1)], a_banks[j % NB]).then_inc(s_evd, 1)
                    if k == 0:
                        for c in range(DC):
                            dve.wait_ge(s_k1, DC * n + c + 1)
                            if r > 0:
                                dve.wait_ge(s_k3, DC * (n - 1) + c + 1)
                            v.tensor_tensor(k_r1[:, c], kf[:, c], kp[par][:, 0, c], ALU.subtract).then_inc(s_kr, 1)
                    if k == 1 and r + 1 < UNITS:
                        split_x(r + 1, it)
                    if k == 2:
                        for c in range(DC):
                            dve.wait_ge(s_k2, DC * n + c + 1)
                            v.tensor_tensor(kp[par][:, 2, c], k_r1[:, c], kp[par][:, 1, c],
                                            ALU.subtract).then_inc(s_k3, 1)

            split_x(0, 0)
            walk(dve, *LOOP_A, project)

            def shifts(r, n):
                dve.wait_ge(s_ln, n)
                steps = 4 * (n - 1)
                v.tensor_tensor(shift[:], negmax[(r - 1) % 2][:], lnden[:], ALU.subtract).then_inc(s_shc, 1)
                dve.wait_ge(s_shc, steps + 1)
                if r >= 2:
                    dve.wait_ge(s_sht, n - 1)
                v.tensor_copy(shift_parts[:, 0], shift[:]).then_inc(s_shc, 1)
                dve.wait_ge(s_shc, steps + 2)
                v.tensor_tensor(shift_r1[:], shift[:], shift_parts[:, 0], ALU.subtract).then_inc(s_shc, 1)
                dve.wait_ge(s_shc, steps + 3)
                v.tensor_copy(shift_parts[:, 1], shift_r1[:]).then_inc(s_shc, 1)
                dve.wait_ge(s_shc, steps + 4)
                v.tensor_tensor(shift_parts[:, 2], shift_r1[:], shift_parts[:, 1], ALU.subtract).then_inc(s_shp, 1)

            def attend(r, it):
                n = r + RING * it
                for u in range(NT):
                    for h in range(2):
                        if r < PAIRS:
                            a = 2 * u + h
                            dve.wait_ge(s_sc, 2 * NT * n + a + 1)
                            v.tensor_reduce(negmax[r % 2][:, NT * h + u:NT * h + u + 1], sc[h][:, 0:P * (u + 1)], AX.X,
                                            ALU.max, negate=True).then_inc(s_max, 1)
                    if u == 0 and 1 <= r <= PAIRS:
                        shifts(r, n)
                    if u == 0 and r >= LAG + 1:
                        copy_o(r - LAG - 1, n - LAG - 1, it)
                    if u == 1 and 1 <= r <= PAIRS:
                        dve.wait_ge(s_sht, n)
                        if r >= 2:
                            dve.wait_ge(s_shd, 16 * (n - 1))
                        v.tensor_copy(shiftT[:], shiftT_ps).then_inc(s_shs, 1)

            def copy_o(r, n, it):
                dve.wait_ge(s_pv, NT * (n + 1))
                if r >= 2:
                    dve.wait_ge(s_ost[r % 2], 16 * (r // 2 + (RING // 2) * it))
                v.tensor_copy(osb[r % 2][:], oo[:]).then_inc(s_oev, 1)

            walk(dve, *LOOP_B, attend)
            copy_o(PAIRS - 1, PAIRS - 1, 0)

            wf_ps, yt_ps, dn_ps = sc[0], sc[1], sc[1]
            up_ps = [st[1][:, :], oo[:, BANK:]]

            def statistics(i, src, made_, count):
                dve.wait_ge(made_, count)
                return v.bn_stats(stats[:, i], src)

            def finish(r, it):
                n = r + 2 * it
                w, f0 = r < UNITS, r >= 1
                if w:
                    dve.wait_ge(s_xn[r % 2], 16 * (r // 2 + it + 1))
                    v.scalar_tensor_tensor(xn[r % 2][:], xn[r % 2][:], 2.0,
                                           bf_sb[:].unsqueeze(1).to_broadcast([P, UT, D]),
                                           ALU.mult, ALU.add).then_inc(s_x2, 1)
                    dve.wait_ge(s_x2, n + 1)
                    if r > 0:
                        dve.wait_ge(s_yn, UT * n)
                    for i in range(UT):
                        dve.wait_ge(s_wf, UT * n + (i | 1) + 1)
                        v.tensor_tensor(y_pre[:, i], wf_ps[:, D * i:D * (i + 1)], xn[r % 2][:, i],
                                        ALU.add).then_inc(s_y, 1)
                if f0:
                    m = n - 1
                    for c in range(DC):
                        dve.wait_ge(s_yh, DC * m + c + 1)
                        v.tensor_tensor(y_lo[:, c], yt_ps[:, BANK * c:BANK * (c + 1)],
                                        y_hi[:, c].bitcast(F32), ALU.subtract).then_inc(s_yl, 1)
                    if r >= 2:
                        dve.wait_ge(s_zn, UT * m)
                        dve.wait_ge(s_dn, UT * m)
                    for f in range(FC):
                        dve.wait_ge(s_si, FC * m + f + 1)
                        v.scalar_tensor_tensor(hT[:, f], up_ps[f % 2], QSCALE, sg[f % 2][:],
                                               ALU.mult, ALU.mult).then_inc(s_h, 1)
                    for i in range(UT):
                        dve.wait_ge(s_dn, UT * m + (i | 1) + 1)
                        v.scalar_tensor_tensor(z_pre[:, i], dn_ps[:, D * i:D * (i + 1)], QSCALE,
                                               y[(r - 1) % 2][:, i], ALU.mult, ALU.add).then_inc(s_z, 1)
                if w:
                    for i in range(UT):
                        statistics(i, y_pre[:, i], s_y, UT * n + i + 1).then_inc(s_bs, 1)
                if f0:
                    for i in range(UT):
                        statistics(UT + i, z_pre[:, i], s_z, UT * (n - 1) + i + 1).then_inc(s_bs, 1)
                a0, a1 = (0 if w else UT), (2 * UT if f0 else UT)
                done = 2 * UT * n - (UT if r >= 1 else 0)
                dve.wait_ge(s_bs, done + a1 - a0)
                settle(dve, s_passed["dve"])
                for a in range(a0, a1):
                    e = v.bn_aggr(mv[:, a], stats[:, a])
                e.then_inc(s_mv, 1)
                dve.wait_ge(s_r0, n + 1)
                sl = slice(a0, a1)
                v.scalar_tensor_tensor(newt[:, 0, sl], mv[:, sl, 1], EPS, rstd0[:, sl],
                                       ALU.add, ALU.mult).then_inc(s_nw, 1)
                dve.wait_ge(s_nw, 4 * n + 1)
                v.tensor_tensor(newt[:, 1, sl], newt[:, 0, sl], rstd0[:, sl], ALU.mult).then_inc(s_nw, 1)
                dve.wait_ge(s_nw, 4 * n + 2)
                v.tensor_scalar(newt[:, 2, sl], newt[:, 1, sl], -0.5, 1.5, ALU.mult, ALU.add).then_inc(s_nw, 1)
                dve.wait_ge(s_nw, 4 * n + 3)
                v.tensor_tensor(rstd[:, sl], newt[:, 2, sl], rstd0[:, sl], ALU.mult).then_inc(s_nw, 1)
                dve.wait_ge(s_nw, 4 * n + 4)
                if w:
                    for i in range(UT):
                        v.tensor_scalar(y[r % 2][:, i], y_pre[:, i], mv[:, i, 0:1], rstd[:, i:i + 1],
                                        ALU.subtract, ALU.mult).then_inc(s_yn, 1)
                if f0:
                    if r >= 3:
                        dve.wait_ge(s_out[(r - 1) % 2], 16 * ((r - 1) // 2 + it))
                    for i in range(UT):
                        a = UT + i
                        v.tensor_scalar(z[(r - 1) % 2][:, i], z_pre[:, i], mv[:, a, 0:1], rstd[:, a:a + 1],
                                        ALU.subtract, ALU.mult).then_inc(s_zn, 1)

            walk(dve, *LOOP_C, finish)


def kernel(**inputs):
    import concourse.bacc as bacc
    import numpy as np
    from concourse.bass_utils import run_bass_kernel_spmd

    a = {k.removeprefix("L0_"): np.asarray(v) for k, v in inputs.items()}
    x = a["attn_x"]
    arrays = {
        "xT": np.ascontiguousarray(x.transpose(0, 2, 1)),
        "x": np.ascontiguousarray(x.reshape(-1, x.shape[-1])),
        "Wk": a["attn_Wk"], "bk": np.ascontiguousarray(a["attn_bk"].reshape(-1, P).T), "Wv": a["attn_Wv"], "bv": np.ascontiguousarray(a["attn_bv"].reshape(-1, P).T),
        "Wf": a["attn_Wf"], "bf": a["attn_bf"],
        "wg": np.ascontiguousarray(a["ffn_w_gate"].T), "wu": np.ascontiguousarray(a["ffn_w_up"].T),
        "wd": np.ascontiguousarray(a["ffn_w_down"].T),
    }
    nc = bacc.Bacc("TRN2", target_bir_lowering=False, num_devices=1)
    args = [nc.dram_tensor(f"in_{n}", v.shape, mybir.dt.from_np(v.dtype), kind="ExternalInput").ap()
            for n, v in arrays.items()]
    out = nc.dram_tensor("out", (x.shape[0] * x.shape[1], x.shape[2]), F32, kind="ExternalOutput").ap()
    build(nc, *args, out)
    r = run_bass_kernel_spmd(nc, [{f"in_{n}": v for n, v in arrays.items()}], core_ids=[0])
    return r.results[0]["out"].reshape(x.shape)
```

```python
from contextlib import ExitStack

import concourse.bass as bass
from concourse import mybir

F32 = mybir.dt.float32
F32R = mybir.dt.float32r
BF16 = mybir.dt.bfloat16
F16 = mybir.dt.float16
I32 = mybir.dt.int32
ALU = mybir.AluOpType
ACT = mybir.ActivationFunctionType
AX = mybir.AxisListType

P = 128
BANK = 512
PARTS = 3
Q_ROWS = (0, 0, 1, 1, 0, 2)
K_ROWS = (0, 1, 0, 1, 2, 0)
MASKED = -1.0e30
EPS = 1.0e-5
HSCALE = 0.125
LN_EXP = "natural_log_exp_and_others"
QSCALE = 1.0 / 127.0


def walk(eng, steps, first, unroll, rounds, body):
    for r in range(first):
        body(r, 0)
    with eng.Fori(0, rounds) as it:
        for k in range(unroll):
            body(first + k, it)
    for r in range(first + unroll * rounds, steps):
        body(r, 0)


def settle(eng, passed):
    eng.sem_inc(passed, 1)


def build(nc, xT, x, Wk, bk, Wv, bv, Wf, bf, wg, wu, wd, out):
    B, D, S = xT.shape
    HV = Wv.shape[1]
    FH = wg.shape[1]
    DH = 16
    H = D // DH
    DV = HV // H
    DC = D // P
    HC = HV // P
    FC = FH // P
    NT = S // P
    PAIRS = B * H // 2
    SPL = len(Q_ROWS) * DH
    ROWS = SPL + PARTS
    U = BANK
    UT = U // P
    UNITS = B * S // U
    assert DH * 8 == P and DV * 2 == P and S == 2 * U and SPL == 96 and UT == 4

    qd = nc.dram_tensor("q_parts", (PARTS, B * D, S), BF16, kind="Internal").ap()
    kd = nc.dram_tensor("k_parts", (PARTS, B * D, S), BF16, kind="Internal").ap()
    vd = nc.dram_tensor("v_pairs", (PAIRS, NT, P, P), F32, kind="Internal").ap()
    od = nc.dram_tensor("o_heads", (B, HV, S), F32, kind="Internal").ap()
    sd = nc.dram_tensor("shifts", (PAIRS, PARTS * 2 * NT, P), BF16, kind="Internal").ap()

    with ExitStack() as ctx:
        def sb(name, shape, dt, c=ctx):
            return c.enter_context(nc.sbuf_tensor(name, shape, dt))

        def sem(name):
            return ctx.enter_context(nc.semaphore(name))

        ident16 = sb("ident16", [P, P], BF16)
        ident32 = sb("ident32", [P, P], F32)
        causal = sb("causal", [P, P], BF16)
        bk_sb = sb("bk_sb", [P, DC], F32)
        bv_sb = sb("bv_sb", [P, HC], F32)
        bf_sb = sb("bf_sb", [P, D], F32)
        eps_sb = sb("eps_sb", [P, 1], F32)
        wk_hi = sb("wk_hi", [P, DC, D], F32R)
        wk_lo = sb("wk_lo", [P, DC, D], F32R)
        wv_hi = sb("wv_hi", [P, DC, HV], F32R)
        wv_lo = sb("wv_lo", [P, DC, HV], F32R)
        wf_sb = sb("wf_sb", [P, HC, D], F32)
        wg_sb = sb("wg_sb", [P, DC, FH], F32R)
        wu_sb = sb("wu_sb", [P, DC, FH], F32R)
        wd_sb = sb("wd_sb", [P, FC, D], F16)

        RING = 4
        Q = [sb(f"q_stack{i}", [ROWS, 2, S], BF16) for i in range(RING)]
        K = [sb(f"k_stack{i}", [ROWS, 2, S], BF16) for i in range(RING)]
        V = [sb(f"v_pair{i}", [P, NT, P], F32) for i in range(RING)]
        negmax = [sb(f"negmax{i}", [P, 2 * NT], F32) for i in range(2)]
        den = [sb(f"den{i}", [P, 2 * NT], F32) for i in range(2)]
        lnden = sb("lnden", [P, 2 * NT], F32)
        shift = sb("shift", [P, 2 * NT], F32)
        shift_r1 = sb("shift_r1", [P, 2 * NT], F32)
        shift_parts = sb("shift_parts", [P, PARTS, 2 * NT], BF16)
        shiftT = sb("shiftT", [PARTS * 2 * NT, P], BF16)
        lctx = ExitStack()
        wk_in = sb("wk_in", [P, DC, D], F32, lctx)
        wv_in = sb("wv_in", [P, DC, HV], F32, lctx)
        wi_in = [sb(f"wi_in{i}", [P, DC * FH], I32, lctx) for i in range(3)]
        lctx.close()
        abctx = ExitStack()
        W = [[sb(f"weights{h}{u}", [P, S - P * u], F32, abctx) for u in range(NT)] for h in range(2)]
        scrap = [sb(f"scrap{h}", [P, S], BF16, abctx) for h in range(2)]
        osb = [sb(f"o_pair{i}", [P, S], F32, abctx) for i in range(2)]
        xt = sb("xt", [P, DC, U], F32, abctx)
        x_hi = sb("x_hi", [P, DC, U], F32R, abctx)
        x_lo = sb("x_lo", [P, DC, U], F32R, abctx)
        qp = sb("q_split", [P, PARTS, DC, U], BF16, abctx)
        kf = sb("kf", [P, DC, U], F32, abctx)
        kp = sb("k_split", [P, PARTS, DC, U], BF16, abctx)
        vs = sb("v_unit", [P, UT, HV], F32, abctx)
        abctx.close()
        y_pre = sb("y_pre", [P, UT, D], F32)
        y = [sb(f"y{i}", [P, UT, D], F32) for i in range(2)]
        y_hi = sb("y_hi", [P, DC, U], F32R)
        y_lo = sb("y_lo", [P, DC, U], F32R)
        sg = [sb(f"silu_gate{i}", [P, U], F32) for i in range(2)]
        h32 = [sb(f"hidden{i}", [P, U], F32) for i in range(2)]
        h_hi = sb("h_hi", [P, FC, U], F16)
        h_lo = sb("h_lo", [P, FC, U], F16)
        z_pre = sb("z_pre", [P, UT, D], F32)
        z = [sb(f"z{i}", [P, UT, D], F32) for i in range(2)]
        g = [sb(f"g{i}", [P, HC, U], F32) for i in range(2)]
        xn = [sb(f"xn{i}", [P, UT, D], F32) for i in range(2)]
        stats = sb("stats", [P, 2 * UT, nc.vector.BN_STATS_DIM], F32)
        mv = sb("mean_var", [P, 2 * UT, 2], F32)
        lnvar = sb("lnvar", [P, 2 * UT], F32)
        rstd0 = sb("rstd0", [P, 2 * UT], F32)
        newt = sb("newton", [P, 3, 2 * UT], F32)
        rstd = sb("rstd", [P, 2 * UT], F32)

        sc = [ctx.enter_context(nc.psum_tensor(f"scores{h}", [P, 2 * BANK], F32)) for h in range(2)]
        st = [ctx.enter_context(nc.psum_tensor(f"scoresT{i}", [P, BANK], F32)) for i in range(2)]
        oo = ctx.enter_context(nc.psum_tensor("o_acc", [P, 2 * BANK], F32))
        a_banks = [sc[0][:, 0:BANK], sc[0][:, BANK:], sc[1][:, 0:BANK], sc[1][:, BANK:], st[0][:, :]]
        shiftT_ps = sc[0][:, BANK:].bitcast(BF16)[0:PARTS * 2 * NT, 0:P]

        s_wkv_in = sem("wkv_loaded")
        s_w_in = sem("other_weights_loaded")
        s_blank = sem("constants_blanked")
        s_const = sem("constants_ready")
        s_w_hi = sem("weights_hi_ready")
        s_wkv = sem("wkv_split")
        s_wrest = sem("ffn_weights_ready")
        s_passed = {e: sem(f"passed_{e}") for e in ("sp", "pool", "pe", "dve")}
        s_xt = sem("xt_loaded")
        s_xhi = sem("x_hi_ready")
        s_xs = sem("x_split")
        s_q1 = sem("q_part1_ready")
        s_qr = sem("q_rest_ready")
        s_q2 = sem("q_part2_ready")
        s_q3 = sem("q_part3_ready")
        s_job = sem("projection_ready")
        s_ev = sem("projection_copied")
        s_k1 = sem("k_part1_ready")
        s_kr = sem("k_rest_ready")
        s_k2 = sem("k_part2_ready")
        s_k3 = sem("k_part3_ready")
        s_qst = sem("q_stored")
        s_kst = sem("k_stored")
        s_vst = [sem(f"v_tile_stored{i}") for i in range(UT)]
        s_stack = [sem(f"stack_loaded{i}") for i in range(RING)]
        s_v = [sem(f"v_loaded{i}") for i in range(RING)]
        s_sc = sem("scores_ready")
        s_max = sem("negmax_ready")
        s_den = sem("den_ready")
        s_ln = sem("lnden_ready")
        s_shc = sem("shift_chain")
        s_shp = sem("shift_parts_ready")
        s_sht = sem("shiftT_ready")
        s_shs = sem("shiftT_copied")
        s_shd = sem("shift_in_dram")
        s_shl = [sem(f"shift_rows_loaded{i}") for i in range(RING)]
        s_st = sem("scoresT_ready")
        s_w = sem("weights_made")
        s_sel = sem("weights_masked")
        s_pv = sem("weights_used")
        s_early = sem("earlier_o_complete")
        s_oev = sem("o_copied")
        s_ost = [sem(f"o_stored{i}") for i in range(2)]
        s_g = [sem(f"g_loaded{i}") for i in range(2)]
        s_xn = [sem(f"xn_loaded{i}") for i in range(2)]
        s_gelu = sem("gelu_done")
        s_wf = sem("wf_ready")
        s_x2 = sem("x_doubled")
        s_y = sem("y_pre_ready")
        s_bs = sem("stats_ready")
        s_mv = sem("mean_var_ready")
        s_lv = sem("lnvar_ready")
        s_r0 = sem("rstd0_ready")
        s_nw = sem("newton_chain")
        s_yn = sem("y_ready")
        s_zn = sem("z_ready")
        s_yt = sem("yT_ready")
        s_yh = sem("y_hi_ready")
        s_yl = sem("y_lo_ready")
        s_gu = sem("gate_up_ready")
        s_si = sem("silu_ready")
        s_h = sem("h_ready")
        s_hh = sem("h_hi_ready")
        s_hl = sem("h_lo_ready")
        s_dn = sem("down_ready")
        s_z = sem("z_pre_ready")
        s_out = [sem(f"out_stored{i}") for i in range(2)]

        block = ctx.enter_context(nc.Block())

        JOBS = [("k", c, 0) for c in range(DC)] + [("v", i, hf) for i in range(UT) for hf in range(2)]
        NB = len(a_banks)
        NJ = len(JOBS)
        SHARE = (range(0, 3), range(3, 6), range(6, 8), range(8, 10))
        b_bank = (oo[:, 0:BANK], sc[1][:, BANK:], oo[:, 0:BANK])
        ALONE = 3

        def unit_beside(r, it):
            a = r // 4 + ALONE
            return a + it if a < UNITS else None

        def jobs_beside(r, it):
            return () if unit_beside(r, it) is None else tuple(enumerate(SHARE[r % 4]))

        def weights(h, u, c0, c1):
            return W[h][u][:, c0 - P * u:c1 - P * u]

        def chunks(u):
            return [(P * u, BANK), (BANK, S)] if P * u < BANK else [(P * u, S)]

        CH = [len(chunks(u)) for u in range(NT)]
        PER_ST = 2 * sum(CH)

        def made(u, h):
            return 2 * sum(CH[:u]) + (CH[u] if h else 0)

        LAG = 2
        BEHIND = 4
        STEPS_B = PAIRS + LAG
        LOOP_B = (STEPS_B, 4, 4, UNITS - ALONE - 2)
        STEPS_C = UNITS + 1
        LOOP_C = (STEPS_C, 3, 2, (UNITS - 6) // 2)

        def unit_of(r, it):
            return r // 2 + it, (r % 2) * U

        @block.sync
        def _(sp):
            sp.dma_start(wk_in[:], Wk.rearrange("(c p) n -> p c n", p=P)).then_inc(s_wkv_in, 16)
            sp.dma_start(wv_in[:], Wv.rearrange("(c p) n -> p c n", p=P)).then_inc(s_wkv_in, 16)
            sp.dma_start(bk_sb[:], bk).then_inc(s_w_in, 16)
            sp.dma_start(bv_sb[:], bv).then_inc(s_w_in, 16)
            sp.dma_start(bf_sb[:], bf.partition_broadcast(P)).then_inc(s_w_in, 16)
            sp.dma_start(wf_sb[:], Wf.rearrange("(c p) n -> p c n", p=P)).then_inc(s_w_in, 16)
            sp.dma_start(wi_in[0][:].rearrange("p (c n) -> p c n", c=DC),
                         wg.rearrange("(c p) n -> p c n", p=P)).then_inc(s_w_in, 16)
            sp.dma_start(wi_in[1][:].rearrange("p (c n) -> p c n", c=DC),
                         wu.rearrange("(c p) n -> p c n", p=P)).then_inc(s_w_in, 16)
            sp.dma_start(wi_in[2][:].rearrange("p (c n) -> p c n", c=FC),
                         wd.rearrange("(c p) n -> p c n", p=P)).then_inc(s_w_in, 16)

            def load_x(a, first=False):
                if not first:
                    sp.wait_ge(s_q3, DC * a)
                    settle(sp, s_passed["sp"])
                sp.dma_start(xt[:], xT[bass.ds(a // 2, 1), :, bass.ds(a % 2 * U, U)].rearrange(
                    "o (c p) t -> (o p) c t", p=P)).then_inc(s_xt, 16)

            def store_parts(parts, split, stored, a):
                for m in range(PARTS):
                    sp.dma_start(parts[m, bass.ds(a // 2 * D, D), bass.ds(a % 2 * U, U)].rearrange(
                        "(c p) t -> p c t", p=P), split[:, m]).then_inc(stored, 16)

            def store_q(a):
                sp.wait_ge(s_q3, DC * (a + 1))
                settle(sp, s_passed["sp"])
                store_parts(qd, qp, s_qst, a)

            def store_k(a):
                sp.wait_ge(s_k3, DC * (a + 1))
                settle(sp, s_passed["sp"])
                store_parts(kd, kp, s_kst, a)

            def store_v(a, i):
                sp.wait_ge(s_ev, NJ * a + DC + 2 * (i + 1))
                settle(sp, s_passed["sp"])
                sp.dma_start(vd[bass.ds(a // 2 * HC, HC), bass.ds(a % 2 * UT + i, 1)].rearrange(
                    "h o t v -> (o t) h v"), vs[:, i].rearrange("t (h v) -> t h v", v=P)
                    ).then_inc(s_vst[i], 16)

            def load_stacks(r, it):
                n = r + RING * it
                slot = r % RING
                if r % 4 == 0:
                    units = min(r // 4 + 2, UNITS) + it
                    for stored, per in ((s_qst, PARTS), (s_kst, PARTS), *((v, 1) for v in s_vst)):
                        sp.wait_ge(stored, 16 * per * units)
                        settle(sp, s_passed["sp"])
                if r >= RING:
                    sp.wait_ge(s_w, PER_ST * (n - RING + 1))
                    settle(sp, s_passed["sp"])
                for (stack, parts, rows) in ((Q, qd, Q_ROWS), (K, kd, K_ROWS)):
                    for i, m in enumerate(rows):
                        sp.dma_start(stack[slot][DH * i:DH * (i + 1), :, :],
                                     parts[m, bass.ds(n * 2 * DH, 2 * DH), :].rearrange(
                                         "(h d) t -> d h t", d=DH)).then_inc(s_stack[slot], 16)

            def load_v(r, it):
                n = r + RING * it
                slot = r % RING
                if r >= RING:
                    sp.wait_ge(s_pv, NT * (n - RING + 1))
                    settle(sp, s_passed["sp"])
                sp.dma_start(V[slot][:], vd[bass.ds(n, 1)].rearrange("o k t v -> (o t) k v")
                             ).then_inc(s_v[slot], 16)

            def attend(r, it):
                n = r + RING * it
                if r + 1 < PAIRS:
                    load_stacks(r + 1, it)
                a, k = unit_beside(r, it), r % 4
                if k == 0 and r > 0 and unit_beside(r - 4, it) is not None:
                    store_v(unit_beside(r - 4, it), UT - 1)
                if a is not None:
                    if k == 1:
                        store_q(a)
                    if k == 2:
                        if r // 4 + ALONE + 1 < UNITS:
                            load_x(a + 1)
                        store_k(a)
                        store_v(a, 0)
                        store_v(a, 1)
                    if k == 3:
                        store_v(a, 2)
                if 1 <= r <= PAIRS:
                    sp.wait_ge(s_shs, n)
                    settle(sp, s_passed["sp"])
                    sp.dma_start(sd[bass.ds(n - 1, 1)].rearrange("o a t -> (o a) t"),
                                 shiftT[:]).then_inc(s_shd, 16)
                    sp.wait_ge(s_shd, 16 * n)
                    settle(sp, s_passed["sp"])
                    slot = (r - 1) % RING
                    sp.dma_start(Q[slot][SPL:ROWS, :, :].rearrange("m h t -> m (h t)"),
                                 sd[bass.ds(n - 1, 1)].rearrange("o (m a) t -> (o m) (a t)", m=PARTS)
                                 ).then_inc(s_shl[slot], 16)
                if r >= LAG + 1:
                    sp.wait_ge(s_oev, 2 * (n - LAG))
                    settle(sp, s_passed["sp"])
                    store_o(r - LAG - 1, n - LAG - 1)
                if r + 1 < PAIRS:
                    load_v(r + 1, it)
                if r == PAIRS - 1:
                    sp.wait_ge(s_job, NJ * UNITS)
                    sp.wait_ge(s_ev, NJ * UNITS)
                    sp.wait_ge(s_k3, DC * UNITS)
                    for i in range(2):
                        sp.wait_ge(s_ost[i], 16 * (PAIRS // B // 2))
                    load_unit(0, 0)
                    load_unit(1, 0)

            def store_o(r, n):
                sp.dma_start(od.rearrange("b h t -> (b h) t")[bass.ds(n * P, P), :],
                             osb[r % 2][:]).then_inc(s_ost[r % 2], 16)

            def load_unit(r, it):
                b, t0 = unit_of(r, it)
                n = r + 2 * it
                if r >= 2:
                    sp.wait_ge(s_wf, UT * (n - 1))
                    settle(sp, s_passed["sp"])
                    sp.wait_ge(s_y, UT * (n - 1))
                    settle(sp, s_passed["sp"])
                sp.dma_start(g[r % 2][:], od[bass.ds(b, 1), :, t0:t0 + U].rearrange(
                    "o (c p) t -> (o p) c t", p=P)).then_inc(s_g[r % 2], 16)
                sp.dma_start(xn[r % 2][:], x[bass.ds(n * U, U), :].rearrange(
                    "(i p) d -> p i d", p=P)).then_inc(s_xn[r % 2], 16)

            load_x(0, True)
            for a in range(ALONE):
                store_q(a)
                load_x(a + 1)
                store_k(a)
                for i in range(UT):
                    store_v(a, i)
                if a == 1:
                    load_stacks(0, 0)
                    load_v(0, 0)
            walk(sp, *LOOP_B, attend)
            sp.wait_ge(s_oev, 2 * PAIRS)
            store_o(PAIRS - 1, PAIRS - 1)
            for i in range(2):
                sp.wait_ge(s_ost[i], 16 * PAIRS // 2)

            def finish(r, it):
                n = r + 2 * it
                if r + 2 < UNITS:
                    load_unit(r + 2, it)
                if r >= 1:
                    sp.wait_ge(s_zn, UT * n)
                    settle(sp, s_passed["sp"])
                    sp.dma_start(out[bass.ds((n - 1) * U, U), :].rearrange("(i p) d -> p i d", p=P),
                                 z[(r - 1) % 2][:]).then_inc(s_out[(r - 1) % 2], 16)

            walk(sp, *LOOP_C, finish)
            for i in range(2):
                sp.wait_ge(s_out[i], 16 * UNITS // 2)

        @block.gpsimd
        def _(pool):
            pool.memset(ident16[:], 0.0).then_inc(s_blank, 1)
            pool.memset(ident32[:], 0.0).then_inc(s_blank, 1)
            pool.memset(causal[:], 0.0).then_inc(s_blank, 1)
            pool.wait_ge(s_blank, 3)
            for m in (ident16, ident32):
                pool.affine_select(out=m[:], in_=m[:], compare_op=ALU.not_equal, fill=1.0, base=0,
                                   pattern=[[-1, P]], channel_multiplier=1).then_inc(s_const, 1)
            pool.affine_select(out=causal[:], in_=causal[:], compare_op=ALU.is_ge, fill=MASKED, base=0,
                               pattern=[[-1, P]], channel_multiplier=1).then_inc(s_const, 1)

            def q_rest(a, c):
                pool.wait_ge(s_xs, a + 1)
                pool.wait_ge(s_q1, DC * a + c + 1)
                pool.tensor_tensor(xt[:, c], xt[:, c], qp[:, 0, c], ALU.subtract).then_inc(s_qr, 1)

            def q_part3(a, c):
                pool.wait_ge(s_q2, DC * a + c + 1)
                pool.tensor_tensor(qp[:, 2, c], xt[:, c], qp[:, 1, c], ALU.subtract).then_inc(s_q3, 1)

            def k_rest(a, c):
                pool.wait_ge(s_k1, DC * a + c + 1)
                pool.tensor_tensor(kf[:, c], kf[:, c], kp[:, 0, c], ALU.subtract).then_inc(s_kr, 1)

            def k_part3(a, c):
                pool.wait_ge(s_k2, DC * a + c + 1)
                pool.tensor_tensor(kp[:, 2, c], kf[:, c], kp[:, 1, c], ALU.subtract).then_inc(s_k3, 1)

            for a in range(ALONE):
                for c in range(DC):
                    q_rest(a, c)
                    q_part3(a, c)
                for c in range(DC):
                    k_rest(a, c)
                    k_part3(a, c)

            def attend(r, it):
                n = r - LAG + RING * it
                a, k = unit_beside(r, it), r % 4
                for u in range(NT):
                    if r >= LAG:
                        for h in range(2):
                            pool.wait_ge(s_w, PER_ST * n + made(u, h) + 1)
                            settle(pool, s_passed["pool"])
                            diag = weights(h, u, P * u, P * (u + 1))
                            pool.affine_select(out=diag, in_=diag, compare_op=ALU.is_ge, fill=0.0, base=0,
                                               pattern=[[1, P]], channel_multiplier=-1).then_inc(s_sel, 1)
                    if a is not None and k < 2:
                        if u in (2, 3):
                            (q_rest if k == 0 else k_rest)(a, u - 2)
                        if u in (6, 7):
                            (q_part3 if k == 0 else k_part3)(a, u - 6)

            walk(pool, *LOOP_B, attend)

            def finish(r, it):
                if r >= 1:
                    m = r - 1 + 2 * it
                    for f in range(FC):
                        pool.wait_ge(s_hh, FC * m + f + 1)
                        pool.tensor_tensor(h_lo[:, f], h32[f % 2][:], h_hi[:, f],
                                           ALU.subtract).then_inc(s_hl, 1)

            walk(pool, *LOOP_C, finish)

        @block.tensor
        def _(pe):
            def mm(o, l, r, start, stop):
                return nc.tensor.matmul(o, l, r, start=start, stop=stop)

            pe.wait_ge(s_wkv, 2)

            def job(j, a, bank, chunks_=range(DC)):
                what, i, hf = JOBS[j]
                last = 3 * DC - 1
                for c in chunks_:
                    if what == "k":
                        cols = slice(P * i, P * (i + 1))
                        terms = ((wk_hi[:, c, cols], x_hi[:, c]), (wk_hi[:, c, cols], x_lo[:, c]),
                                 (wk_lo[:, c, cols], x_hi[:, c]))
                    else:
                        toks, cols = slice(P * i, P * (i + 1)), slice(BANK * hf, BANK * (hf + 1))
                        terms = ((x_hi[:, c, toks], wv_hi[:, c, cols]), (x_hi[:, c, toks], wv_lo[:, c, cols]),
                                 (x_lo[:, c, toks], wv_hi[:, c, cols]))
                    for k, (l, m) in enumerate(terms):
                        e = mm(bank, l, m, 3 * c + k == 0, 3 * c + k == last)
                if chunks_[-1] == DC - 1:
                    e.then_inc(s_job, 1)

            for a in range(ALONE):
                pe.wait_ge(s_xs, a + 1)
                for j in range(NJ):
                    if NJ * a + j >= NB:
                        pe.wait_ge(s_ev, NJ * a + j - NB + 1)
                    job(j, a, a_banks[(NJ * a + j) % NB])
            pe.wait_ge(s_ev, NJ * ALONE)
            pe.wait_ge(s_const, 3 + RING + 1)

            def job_beside(r, it, i, chunk):
                for place, j in jobs_beside(r, it):
                    if place == i:
                        a = unit_beside(r, it)
                        if j == 0 and chunk == 0:
                            pe.wait_ge(s_xs, a + 1)
                        if i == 0 and chunk == 0 and r >= LAG + 1:
                            pe.wait_ge(s_oev, 2 * (r - LAG - 1 + RING * it) + 1)
                        if i == 2 and chunk == 0:
                            pe.wait_ge(s_ev, NJ * a + j - 1)
                        job(j, a, b_bank[i], range(chunk, chunk + 1))

            def score(h, u, r, n):
                q, k = Q[r % RING], K[r % RING]
                if u > 0 or r > 0:
                    pe.wait_ge(s_den, 2 * NT * n + 2 * u + h - 1)
                width = P * (u + 1)
                for c0 in range(0, width, BANK):
                    c1 = min(width, c0 + BANK)
                    mm(sc[h][:, c0:c1], q[0:SPL, h, P * u:P * (u + 1)], k[0:SPL, h, c0:c1], True, c1 < width)
                mm(sc[h][:, width - P:width], ident16[:], causal[:], False, True).then_inc(s_sc, 1)

            def scoreT(h, u, r, n):
                q, k = Q[r % RING], K[r % RING]
                for i, (c0, c1) in enumerate(chunks(u)):
                    c = made(u, h) + i
                    if r > 0 or c >= 2:
                        pe.wait_ge(s_w, PER_ST * n + c - 1)
                    mm(st[c % 2][:, 0:c1 - c0], k[:, h, P * u:P * (u + 1)], q[:, h, c0:c1],
                       True, True).then_inc(s_st, 1)

            def weigh(u, r, it, chunk):
                n = r + RING * it
                if chunk == 0:
                    if u == 0:
                        pe.wait_ge(s_v[r % RING], 16 * (r // RING + it + 1))
                    pe.wait_ge(s_w, PER_ST * n + made(u + 1, 0))
                    pe.wait_ge(s_sel, 2 * NT * n + 2 * (u + 1))
                if u == 0 and r > 0:
                    pe.wait_ge(s_oev, 2 * n - 1 + chunk)
                for (c0, c1) in chunks(u)[chunk:chunk + 1]:
                    for h in range(2):
                        e = mm(oo[DV * h:DV * (h + 1), c0:c1], V[r % RING][:, u, DV * h:DV * (h + 1)],
                               weights(h, u, c0, c1), u == 0, P * (u + 1) == c1)
                    if u == NT // 2 - 1 and c1 == BANK:
                        e.then_inc(s_early, 1)
                    if chunk == CH[u] - 1:
                        e.then_inc(s_pv, 1)

            def weigh_behind(u, r, it, chunk):
                u, pair = (u - BEHIND, r - LAG) if u >= BEHIND else (u - BEHIND + NT, r - LAG - 1)
                if 0 <= pair < PAIRS:
                    weigh(u, pair, it, chunk)

            def open_pair(r, it):
                pe.wait_ge(s_stack[r % RING], 16 * (len(Q_ROWS) + len(K_ROWS)) * (r // RING + it + 1))

            def attend(r, it):
                n = r + RING * it
                weighing = r >= LAG
                m, rm = n - LAG, r - LAG
                for u in range(NT):
                    if u == 2 and 1 <= r <= PAIRS:
                        pe.wait_ge(s_shp, n)
                        settle(pe, s_passed["pe"])
                        nc.tensor.transpose(shiftT_ps, shift_parts[:].rearrange("p m a -> p (m a)"),
                                            ident16[:]).then_inc(s_sht, 1)
                    if u == 3 and 1 <= r < PAIRS:
                        pe.wait_ge(s_shs, n)
                    a, share = unit_beside(r, it), SHARE[r % 4]
                    if u == BEHIND and a is not None:
                        pe.wait_ge(s_ev, NJ * a + share[-1] + 1)

                    def next_score(h):
                        if u + 1 < NT and r < PAIRS:
                            score(h, u + 1, r, n)
                        elif u + 1 == NT and r + 1 < PAIRS:
                            if h == 0:
                                open_pair(r + 1, it)
                            score(h, 0, r + 1, n + 1)

                    next_score(0)
                    if weighing:
                        scoreT(1, u, rm, m)
                    weigh_behind(u, r, it, 0)
                    if u >= 1:
                        job_beside(r, it, u - 1, 1)
                    if u == 3 and a is not None:
                        pe.wait_ge(s_ev, NJ * a + share[1] + 1)
                    next_score(1)
                    if u + 1 < NT and weighing:
                        scoreT(0, u + 1, rm, m)
                    if u + 1 == NT and LAG <= r + 1 < STEPS_B:
                        pe.wait_ge(s_shl[(rm + 1) % RING], 16 * ((rm + 1) // RING + it + 1))
                        scoreT(0, 0, rm + 1, m + 1)
                    weigh_behind(u, r, it, 1)
                    job_beside(r, it, u, 0)

            open_pair(0, 0)
            score(0, 0, 0, 0)
            score(1, 0, 0, 0)
            walk(pe, *LOOP_B, attend)
            for u in range(BEHIND):
                weigh_behind(u, STEPS_B, 0, 0)
            pe.wait_ge(s_oev, 2 * PAIRS)
            pe.wait_ge(s_wrest, 3)

            wf_ps, yt_ps, dn_ps = sc[0], sc[1], sc[1]
            gate_ps = [st[0][:, :], oo[:, 0:BANK]]
            up_ps = [st[1][:, :], oo[:, BANK:]]

            def wf_product(r, n, tiles):
                for i in tiles:
                    if i == 0 and r > 0:
                        pe.wait_ge(s_y, UT * n)
                    for c in range(HC):
                        if i == 0:
                            pe.wait_ge(s_gelu, HC * n + c + 1)
                        e = mm(wf_ps[:, D * i:D * (i + 1)], g[r % 2][:, c, P * i:P * (i + 1)], wf_sb[:, c],
                               c == 0, c == HC - 1)
                    e.then_inc(s_wf, 1)

            def transpose_y(r, m):
                if r > 0:
                    pe.wait_ge(s_z, UT * m)
                for i in range(UT):
                    pe.wait_ge(s_yn, UT * m + i + 1)
                    for c in range(DC):
                        e = nc.tensor.transpose(yt_ps[:, BANK * c + P * i:BANK * c + P * (i + 1)],
                                                y[r % 2][:, i, P * c:P * (c + 1)], ident32[:])
                e.then_inc(s_yt, 1)

            def gate_up(r, m):
                pe.wait_ge(s_yl, DC * (m + 1))
                for f in range(FC):
                    if r > 0 or f >= 2:
                        pe.wait_ge(s_h, FC * m + f - 1)
                    cols = slice(P * f, P * (f + 1))
                    for ps, w in ((gate_ps[f % 2], wg_sb), (up_ps[f % 2], wu_sb)):
                        for c in range(DC):
                            for k, part in enumerate((y_hi, y_lo)):
                                e = mm(ps, w[:, c, cols], part[:, c], c + k == 0, c == DC - 1 and k == 1)
                    e.then_inc(s_gu, 1)

            def down(m):
                for i in range(UT):
                    for f in range(FC):
                        if i == 0:
                            pe.wait_ge(s_hl, FC * m + f + 1)
                        for k, part in enumerate((h_hi, h_lo)):
                            e = mm(dn_ps[:, D * i:D * (i + 1)], part[:, f, P * i:P * (i + 1)], wd_sb[:, f],
                                   f + k == 0, f == FC - 1 and k == 1)
                    e.then_inc(s_dn, 1)

            def finish(r, it):
                n = r + 2 * it
                if r < UNITS:
                    wf_product(r, n, (0, 1))
                if r >= 1:
                    transpose_y(r - 1, n - 1)
                if r < UNITS:
                    wf_product(r, n, (2,))
                if r >= 1:
                    gate_up(r - 1, n - 1)
                if r < UNITS:
                    wf_product(r, n, (3,))
                if r >= 1:
                    down(n - 1)

            walk(pe, *LOOP_C, finish)

        @block.scalar
        def _(act):
            def copy(o, i):
                return nc.scalar.activation(o, i, ACT.Copy)

            act.preload_act_table_set(LN_EXP)
            act.wait_ge(s_wkv, 2)
            act.wait_ge(s_wrest, 3)
            act.wait_ge(s_const, 3 + RING + 1)

            def attend(r, it):
                n = r + RING * it
                if 1 <= r <= PAIRS:
                    act.wait_ge(s_den, 2 * NT * n)
                    if r >= 2:
                        act.wait_ge(s_shp, n - 1)
                    nc.scalar.activation(lnden[:], den[(r - 1) % 2][:], ACT.Ln).then_inc(s_ln, 1)
                if r >= 2 and r < PAIRS:
                    act.wait_ge(s_shp, n - 1)
                for u in range(NT):
                    for h in range(2):
                        if r < PAIRS:
                            a = 2 * u + h
                            act.wait_ge(s_max, 2 * NT * n + a + 1)
                            width = P * (u + 1)
                            nc.scalar.activation(scrap[h][:, 0:width], sc[h][:, 0:width], ACT.Exp,
                                                 bias=negmax[r % 2][:, NT * h + u:NT * h + u + 1],
                                                 accum_out=den[r % 2][:, NT * h + u:NT * h + u + 1]
                                                 ).then_inc(s_den, 1)
                        if r >= LAG:
                            m, rm = n - LAG, r - LAG
                            for i, (c0, c1) in enumerate(chunks(u)):
                                c = made(u, h) + i
                                act.wait_ge(s_st, PER_ST * m + c + 1)
                                if i == 0 and rm > 0:
                                    act.wait_ge(s_pv, NT * (m - 1) + u + 1)
                                nc.scalar.activation(weights(h, u, c0, c1), st[c % 2][:, 0:c1 - c0],
                                                     ACT.Exp).then_inc(s_w, 1)

            walk(act, *LOOP_B, attend)

            def gelus(r, n, stored):
                act.wait_ge(s_g[r % 2], 16 * (stored + 1))
                for c in range(HC):
                    nc.scalar.activation(g[r % 2][:, c], g[r % 2][:, c], ACT.Gelu,
                                         bias=bv_sb[:, c:c + 1]).then_inc(s_gelu, 1)

            gate_ps = [st[0][:, :], oo[:, 0:BANK]]
            gelus(0, 0, 0)

            def finish(r, it):
                n = r + 2 * it
                if r >= 1:
                    m = n - 1
                    act.wait_ge(s_yt, m + 1)
                    for c in range(DC):
                        copy(y_hi[:, c], sc[1][:, BANK * c:BANK * (c + 1)]).then_inc(s_yh, 1)
                    for f in range(FC + 1):
                        if f < FC:
                            act.wait_ge(s_gu, FC * m + f + 1)
                            nc.scalar.activation(sg[f % 2][:], gate_ps[f % 2], ACT.Silu,
                                                 scale=QSCALE).then_inc(s_si, 1)
                        if f > 0:
                            if f == 1 and r >= 2:
                                act.wait_ge(s_dn, UT * m)
                            act.wait_ge(s_h, FC * m + f)
                            copy(h_hi[:, f - 1], h32[(f - 1) % 2][:]).then_inc(s_hh, 1)
                if r + 1 < UNITS:
                    gelus(r + 1, n + 1, (r + 1) // 2 + it)
                a0, a1 = (0 if r < UNITS else UT), (2 * UT if r >= 1 else UT)
                act.preload_act_table_set(LN_EXP)
                act.wait_ge(s_mv, n + 1)
                nc.scalar.activation(lnvar[:, a0:a1], mv[:, a0:a1, 1], ACT.Ln, bias=eps_sb[:]).then_inc(s_lv, 1)
                act.wait_ge(s_lv, n + 1)
                nc.scalar.activation(rstd0[:, a0:a1], lnvar[:, a0:a1], ACT.Exp, scale=-0.5).then_inc(s_r0, 1)

            walk(act, *LOOP_C, finish)

        @block.vector
        def _(dve):
            v = nc.vector
            for i in range(RING):
                v.memset(K[i][SPL:ROWS, :, :], 1.0).then_inc(s_const, 1)
            v.memset(eps_sb[:], EPS).then_inc(s_const, 1)

            dve.wait_ge(s_wkv_in, 32)
            v.tensor_copy(wk_hi[:], wk_in[:]).then_inc(s_w_hi, 1)
            v.tensor_copy(wv_hi[:], wv_in[:]).then_inc(s_w_hi, 1)
            dve.wait_ge(s_w_hi, 2)
            v.tensor_tensor(wk_lo[:], wk_in[:], wk_hi[:].bitcast(F32), ALU.subtract).then_inc(s_wkv, 1)
            v.tensor_tensor(wv_lo[:], wv_in[:], wv_hi[:].bitcast(F32), ALU.subtract).then_inc(s_wkv, 1)
            dve.wait_ge(s_w_in, 16 * 7)
            for dst, src in ((wg_sb, wi_in[0]), (wu_sb, wi_in[1]), (wd_sb, wi_in[2])):
                v.tensor_copy(dst[:].rearrange("p c n -> p (c n)"), src[:]).then_inc(s_wrest, 1)

            def x_part1(a, first=False):
                dve.wait_ge(s_xt, 16 * (a + 1))
                if not first:
                    dve.wait_ge(s_job, NJ * a)
                v.tensor_copy(x_hi[:], xt[:]).then_inc(s_xhi, 1)

            def x_part2(a):
                dve.wait_ge(s_xhi, a + 1)
                v.tensor_tensor(x_lo[:], xt[:], x_hi[:].bitcast(F32), ALU.subtract).then_inc(s_xs, 1)

            def q_part1(a, first=False):
                if not first:
                    dve.wait_ge(s_qst, 16 * PARTS * a)
                for c in range(DC):
                    v.tensor_copy(qp[:, 0, c], xt[:, c]).then_inc(s_q1, 1)

            def q_part2(a, c):
                dve.wait_ge(s_qr, DC * a + c + 1)
                v.tensor_copy(qp[:, 1, c], xt[:, c]).then_inc(s_q2, 1)

            def k_part2(a, c):
                dve.wait_ge(s_kr, DC * a + c + 1)
                v.tensor_copy(kp[:, 1, c], kf[:, c]).then_inc(s_k2, 1)

            def copy_out(j, a, bank, first=False):
                what, i, hf = JOBS[j]
                dve.wait_ge(s_job, NJ * a + j + 1)
                if what == "k":
                    if not first:
                        dve.wait_ge(s_k3, DC * (a - 1) + i + 1)
                        dve.wait_ge(s_kst, 16 * PARTS * a)
                    v.tensor_scalar(kf[:, i], bank, bk_sb[:, i:i + 1], None, ALU.add).then_inc(s_ev, 1)
                    dve.wait_ge(s_ev, NJ * a + j + 1)
                    v.tensor_copy(kp[:, 0, i], kf[:, i]).then_inc(s_k1, 1)
                else:
                    if not first and hf == 0:
                        dve.wait_ge(s_vst[i], 16 * a)
                    v.tensor_copy(vs[:, i, BANK * hf:BANK * (hf + 1)], bank).then_inc(s_ev, 1)

            x_part1(0, True)
            x_part2(0)
            q_part1(0, True)
            for a in range(ALONE):
                for j in range(NJ):
                    copy_out(j, a, a_banks[(NJ * a + j) % NB], a == 0)
                    if j in (2, 3):
                        q_part2(a, j - 2)
                    if j in (5, 6):
                        k_part2(a, j - 5)
                x_part1(a + 1)
                x_part2(a + 1)
                if a + 1 < ALONE:
                    q_part1(a + 1)

            def shifts(r, n, step):
                if step == 0:
                    dve.wait_ge(s_ln, n)
                else:
                    dve.wait_ge(s_shc, 4 * (n - 1) + step)
                if step == 0:
                    v.tensor_tensor(shift[:], negmax[(r - 1) % 2][:], lnden[:], ALU.subtract).then_inc(s_shc, 1)
                if step == 1:
                    if r >= 2:
                        dve.wait_ge(s_sht, n - 1)
                    v.tensor_copy(shift_parts[:, 0], shift[:]).then_inc(s_shc, 1)
                if step == 2:
                    v.tensor_tensor(shift_r1[:], shift[:], shift_parts[:, 0], ALU.subtract).then_inc(s_shc, 1)
                if step == 3:
                    v.tensor_copy(shift_parts[:, 1], shift_r1[:]).then_inc(s_shc, 1)
                if step == 4:
                    v.tensor_tensor(shift_parts[:, 2], shift_r1[:], shift_parts[:, 1],
                                    ALU.subtract).then_inc(s_shp, 1)

            def attend(r, it):
                n = r + RING * it
                a, k = unit_beside(r, it), r % 4
                for u in range(NT):
                    for h in range(2):
                        if r < PAIRS:
                            dve.wait_ge(s_sc, 2 * NT * n + 2 * u + h + 1)
                            v.tensor_reduce(negmax[r % 2][:, NT * h + u:NT * h + u + 1], sc[h][:, 0:P * (u + 1)],
                                            AX.X, ALU.max, negate=True).then_inc(s_max, 1)
                        if 2 * u + h < 5 and 1 <= r <= PAIRS:
                            shifts(r, n, 2 * u + h)
                        if h == 0 and u == 3 and 1 <= r <= PAIRS:
                            dve.wait_ge(s_sht, n)
                            if r >= 2:
                                dve.wait_ge(s_shd, 16 * (n - 1))
                            v.tensor_copy(shiftT[:], shiftT_ps).then_inc(s_shs, 1)
                        if h == 0:
                            for i, j in jobs_beside(r, it):
                                if i + 2 == u:
                                    copy_out(j, a, b_bank[i])
                            if u in (1, BEHIND + 1) and r >= LAG + 1:
                                copy_o(0 if u == 1 else 1, r - LAG - 1, n - LAG - 1, it)
                    if a is not None:
                        if k == 0 and u == 1:
                            q_part1(a)
                        if k == 0 and u in (5, 6):
                            q_part2(a, u - 5)
                        if k == 1 and u in (5, 6):
                            k_part2(a, u - 5)
                        if k == 3 and u in (3, 5) and r // 4 + ALONE + 1 < UNITS:
                            (x_part1 if u == 3 else x_part2)(a + 1)

            def copy_o(half, r, n, it):
                if half:
                    dve.wait_ge(s_pv, NT * (n + 1))
                else:
                    dve.wait_ge(s_early, n + 1)
                if half == 0 and r >= 2:
                    dve.wait_ge(s_ost[r % 2], 16 * (r // 2 + (RING // 2) * it))
                cols = slice(BANK * half, BANK * (half + 1))
                v.tensor_copy(osb[r % 2][:, cols], oo[:, cols]).then_inc(s_oev, 1)

            walk(dve, *LOOP_B, attend)
            for half in range(2):
                copy_o(half, PAIRS - 1, PAIRS - 1, 0)
            for i in range(2):
                dve.wait_ge(s_ost[i], 16 * PAIRS // 2)

            wf_ps, yt_ps, dn_ps = sc[0], sc[1], sc[1]
            up_ps = [st[1][:, :], oo[:, BANK:]]

            def statistics(i, src, made_, count):
                dve.wait_ge(made_, count)
                return v.bn_stats(stats[:, i], src)

            def finish(r, it):
                n = r + 2 * it
                w, f0 = r < UNITS, r >= 1
                if w:
                    dve.wait_ge(s_xn[r % 2], 16 * (r // 2 + it + 1))
                    v.scalar_tensor_tensor(xn[r % 2][:], xn[r % 2][:], 2.0,
                                           bf_sb[:].unsqueeze(1).to_broadcast([P, UT, D]),
                                           ALU.mult, ALU.add).then_inc(s_x2, 1)
                    dve.wait_ge(s_x2, n + 1)
                    if r > 0:
                        dve.wait_ge(s_yn, UT * n)

                def add_x(tiles):
                    for i in tiles:
                        dve.wait_ge(s_wf, UT * n + (i | 1) + 1)
                        v.tensor_tensor(y_pre[:, i], wf_ps[:, D * i:D * (i + 1)], xn[r % 2][:, i],
                                        ALU.add).then_inc(s_y, 1)

                if w:
                    add_x((0, 1))
                if f0:
                    m = n - 1
                    for c in range(DC):
                        dve.wait_ge(s_yh, DC * m + c + 1)
                        v.tensor_tensor(y_lo[:, c], yt_ps[:, BANK * c:BANK * (c + 1)],
                                        y_hi[:, c].bitcast(F32), ALU.subtract).then_inc(s_yl, 1)
                    if r >= 2:
                        dve.wait_ge(s_zn, UT * m)
                    for f in range(FC):
                        dve.wait_ge(s_si, FC * m + f + 1)
                        if r >= 2 or f >= 2:
                            dve.wait_ge(s_hl, FC * m + f - 1)
                        v.scalar_tensor_tensor(h32[f % 2][:], up_ps[f % 2], QSCALE * HSCALE, sg[f % 2][:],
                                               ALU.mult, ALU.mult).then_inc(s_h, 1)
                if w:
                    add_x((2, 3))
                if f0:
                    for i in range(UT):
                        dve.wait_ge(s_dn, UT * m + (i | 1) + 1)
                        v.scalar_tensor_tensor(z_pre[:, i], dn_ps[:, D * i:D * (i + 1)], QSCALE / HSCALE,
                                               y[(r - 1) % 2][:, i], ALU.mult, ALU.add).then_inc(s_z, 1)
                if w:
                    for i in range(UT):
                        statistics(i, y_pre[:, i], s_y, UT * n + i + 1).then_inc(s_bs, 1)
                if f0:
                    for i in range(UT):
                        statistics(UT + i, z_pre[:, i], s_z, UT * (n - 1) + i + 1).then_inc(s_bs, 1)
                a0, a1 = (0 if w else UT), (2 * UT if f0 else UT)
                done = 2 * UT * n - (UT if r >= 1 else 0)
                dve.wait_ge(s_bs, done + a1 - a0)
                settle(dve, s_passed["dve"])
                for a in range(a0, a1):
                    e = v.bn_aggr(mv[:, a], stats[:, a])
                e.then_inc(s_mv, 1)
                dve.wait_ge(s_r0, n + 1)
                sl = slice(a0, a1)
                v.scalar_tensor_tensor(newt[:, 0, sl], mv[:, sl, 1], EPS, rstd0[:, sl],
                                       ALU.add, ALU.mult).then_inc(s_nw, 1)
                dve.wait_ge(s_nw, 4 * n + 1)
                v.tensor_tensor(newt[:, 1, sl], newt[:, 0, sl], rstd0[:, sl], ALU.mult).then_inc(s_nw, 1)
                dve.wait_ge(s_nw, 4 * n + 2)
                v.tensor_scalar(newt[:, 2, sl], newt[:, 1, sl], -0.5, 1.5, ALU.mult, ALU.add).then_inc(s_nw, 1)
                dve.wait_ge(s_nw, 4 * n + 3)
                v.tensor_tensor(rstd[:, sl], newt[:, 2, sl], rstd0[:, sl], ALU.mult).then_inc(s_nw, 1)
                dve.wait_ge(s_nw, 4 * n + 4)
                if w:
                    for i in range(UT):
                        v.tensor_scalar(y[r % 2][:, i], y_pre[:, i], mv[:, i, 0:1], rstd[:, i:i + 1],
                                        ALU.subtract, ALU.mult).then_inc(s_yn, 1)
                if f0:
                    if r >= 3:
                        dve.wait_ge(s_out[(r - 1) % 2], 16 * ((r - 1) // 2 + it))
                    for i in range(UT):
                        a = UT + i
                        v.tensor_scalar(z[(r - 1) % 2][:, i], z_pre[:, i], mv[:, a, 0:1], rstd[:, a:a + 1],
                                        ALU.subtract, ALU.mult).then_inc(s_zn, 1)

            walk(dve, *LOOP_C, finish)


def kernel(**inputs):
    import concourse.bacc as bacc
    import numpy as np
    from concourse.bass_utils import run_bass_kernel_spmd

    a = {k.removeprefix("L0_"): np.asarray(v) for k, v in inputs.items()}
    x = a["attn_x"]
    arrays = {
        "xT": np.ascontiguousarray(x.transpose(0, 2, 1)),
        "x": np.ascontiguousarray(x.reshape(-1, x.shape[-1])),
        "Wk": a["attn_Wk"], "bk": np.ascontiguousarray(a["attn_bk"].reshape(-1, P).T), "Wv": a["attn_Wv"], "bv": np.ascontiguousarray(a["attn_bv"].reshape(-1, P).T),
        "Wf": a["attn_Wf"], "bf": a["attn_bf"],
        "wg": np.ascontiguousarray(a["ffn_w_gate"].T), "wu": np.ascontiguousarray(a["ffn_w_up"].T),
        "wd": np.ascontiguousarray(a["ffn_w_down"].T),
    }
    nc = bacc.Bacc("TRN2", target_bir_lowering=False, num_devices=1)
    args = [nc.dram_tensor(f"in_{n}", v.shape, mybir.dt.from_np(v.dtype), kind="ExternalInput").ap()
            for n, v in arrays.items()]
    out = nc.dram_tensor("out", (x.shape[0] * x.shape[1], x.shape[2]), F32, kind="ExternalOutput").ap()
    build(nc, *args, out)
    r = run_bass_kernel_spmd(nc, [{f"in_{n}": v for n, v in arrays.items()}], core_ids=[0])
    return r.results[0]["out"].reshape(x.shape)
```

```python
from contextlib import ExitStack

import concourse.bass as bass
from concourse import mybir

F32 = mybir.dt.float32
F32R = mybir.dt.float32r
BF16 = mybir.dt.bfloat16
F16 = mybir.dt.float16
I32 = mybir.dt.int32
ALU = mybir.AluOpType
ACT = mybir.ActivationFunctionType
AX = mybir.AxisListType

P = 128
BANK = 512
PARTS = 3
Q_ROWS = (0, 0, 1, 1, 0, 2)
K_ROWS = (0, 1, 0, 1, 2, 0)
MASKED = -1.0e30
EPS = 1.0e-5
HSCALE = 0.125
SQ = 32
LN_EXP = "natural_log_exp_and_others"
QSCALE = 1.0 / 127.0


def walk(eng, steps, first, unroll, rounds, body):
    for r in range(first):
        body(r, 0)
    with eng.Fori(0, rounds) as it:
        for k in range(unroll):
            body(first + k, it)
    for r in range(first + unroll * rounds, steps):
        body(r, 0)


def settle(eng, passed):
    eng.sem_inc(passed, 1)


def build(nc, xT, x, Wk, bk, Wv, bv, Wf, bf, wg, wu, wd, out):
    B, D, S = xT.shape
    HV = Wv.shape[1]
    FH = wg.shape[1]
    DH = 16
    H = D // DH
    DV = HV // H
    DC = D // P
    HC = HV // P
    FC = FH // P
    NT = S // P
    PAIRS = B * H // 2
    SPL = len(Q_ROWS) * DH
    ROWS = SPL + PARTS
    U = BANK
    UT = U // P
    UNITS = B * S // U
    assert DH * 8 == P and DV * 2 == P and S == 2 * U and SPL == 96 and UT == 4

    qd = nc.dram_tensor("q_parts", (PARTS, B * D, S), BF16, kind="Internal").ap()
    kd = nc.dram_tensor("k_parts", (PARTS, B * D, S), BF16, kind="Internal").ap()
    vd = nc.dram_tensor("v_pairs", (PAIRS, NT, P, P), F32, kind="Internal").ap()
    od = nc.dram_tensor("o_heads", (B, HV, S), F32, kind="Internal").ap()
    sd = nc.dram_tensor("shifts", (PAIRS, P, (PARTS + 1) * 2 * NT), BF16, kind="Internal").ap()

    with ExitStack() as ctx:
        def sb(name, shape, dt, c=ctx):
            return c.enter_context(nc.sbuf_tensor(name, shape, dt))

        def sem(name):
            return ctx.enter_context(nc.semaphore(name))

        ident16 = sb("ident16", [P, P], BF16)
        ident32 = sb("ident32", [P, P], F32)
        causal = sb("causal", [P, P], BF16)
        bk_sb = sb("bk_sb", [P, DC], F32)
        bv_sb = sb("bv_sb", [P, HC], F32)
        bf_sb = sb("bf_sb", [P, D], F32)
        eps_sb = sb("eps_sb", [P, 1], F32)
        wk_hi = sb("wk_hi", [P, DC, D], F32R)
        wk_lo = sb("wk_lo", [P, DC, D], F32R)
        wv_hi = sb("wv_hi", [P, DC, HV], F32R)
        wv_lo = sb("wv_lo", [P, DC, HV], F32R)
        wf_sb = sb("wf_sb", [P, HC, D], F32)
        wg_sb = sb("wg_sb", [P, DC, FH], F32R)
        wu_sb = sb("wu_sb", [P, DC, FH], F32R)
        wd_sb = sb("wd_sb", [P, FC, D], F16)

        RING = 4
        Q = [sb(f"q_stack{i}", [ROWS, 2, S], BF16) for i in range(RING)]
        K = [sb(f"k_stack{i}", [ROWS, 2, S], BF16) for i in range(RING)]
        V = [sb(f"v_pair{i}", [P, NT, P], F32) for i in range(RING)]
        negmax = [sb(f"negmax{i}", [P, 2 * NT], F32) for i in range(2)]
        den = [sb(f"den{i}", [P, 2 * NT], F32) for i in range(2)]
        lnden = sb("lnden", [P, 2 * NT], F32)
        shift = sb("shift", [P, 2 * NT], F32)
        shift_r1 = sb("shift_r1", [P, 2 * NT], F32)
        shift_parts = sb("shift_parts", [P, PARTS + 1, 2 * NT], BF16)
        shiftT = sb("shiftT", [P, PARTS + 1, 2 * NT], BF16)
        lctx = ExitStack()
        wk_in = sb("wk_in", [P, DC, D], F32, lctx)
        wv_in = sb("wv_in", [P, DC, HV], F32, lctx)
        wi_in = [sb(f"wi_in{i}", [P, DC * FH], I32, lctx) for i in range(3)]
        lctx.close()
        abctx = ExitStack()
        W = [[sb(f"weights{h}{u}", [P, S - P * u], F32, abctx) for u in range(NT)] for h in range(2)]
        scrap = [sb(f"scrap{h}", [P, S], BF16, abctx) for h in range(2)]
        osb = [sb(f"o_pair{i}", [P, S], F32, abctx) for i in range(2)]
        xt = sb("xt", [P, DC, U], F32, abctx)
        x_hi = sb("x_hi", [P, DC, U], F32R, abctx)
        x_lo = sb("x_lo", [P, DC, U], F32R, abctx)
        qp = sb("q_split", [P, PARTS, DC, U], BF16, abctx)
        kf = sb("kf", [P, DC, U], F32, abctx)
        kp = sb("k_split", [P, PARTS, DC, U], BF16, abctx)
        vs = sb("v_unit", [P, UT, HV], F32, abctx)
        abctx.close()
        y_pre = sb("y_pre", [P, UT, D], F32)
        y = [sb(f"y{i}", [P, UT, D], F32) for i in range(2)]
        y_hi = sb("y_hi", [P, DC, U], F32R)
        y_lo = sb("y_lo", [P, DC, U], F32R)
        sg = [sb(f"silu_gate{i}", [P, U], F32) for i in range(2)]
        h32 = [sb(f"hidden{i}", [P, U], F32) for i in range(2)]
        h_hi = sb("h_hi", [P, FC, U], F16)
        h_lo = sb("h_lo", [P, FC, U], F16)
        z_pre = sb("z_pre", [P, UT, D], F32)
        z = [sb(f"z{i}", [P, UT, D], F32) for i in range(2)]
        g = [sb(f"g{i}", [P, HC, U], F32) for i in range(2)]
        xn = [sb(f"xn{i}", [P, UT, D], F32) for i in range(2)]
        stats = sb("stats", [P, 2 * UT, nc.vector.BN_STATS_DIM], F32)
        mv = sb("mean_var", [P, 2 * UT, 2], F32)
        lnvar = sb("lnvar", [P, 2 * UT], F32)
        rstd0 = sb("rstd0", [P, 2 * UT], F32)
        newt = sb("newton", [P, 3, 2 * UT], F32)
        rstd = sb("rstd", [P, 2 * UT], F32)

        sc = [ctx.enter_context(nc.psum_tensor(f"scores{h}", [P, 2 * BANK], F32)) for h in range(2)]
        st = [ctx.enter_context(nc.psum_tensor(f"scoresT{i}", [P, BANK], F32)) for i in range(2)]
        oo = ctx.enter_context(nc.psum_tensor("o_acc", [P, 2 * BANK], F32))
        a_banks = [sc[0][:, 0:BANK], sc[0][:, BANK:], sc[1][:, 0:BANK], sc[1][:, BANK:], st[0][:, :]]

        s_wk_in = sem("wk_loaded")
        s_wv_in = sem("wv_loaded")
        s_bk = sem("bk_loaded")
        s_w_in = sem("other_weights_loaded")
        s_blank = sem("constants_blanked")
        s_const = sem("constants_ready")
        s_w_hi = sem("weights_hi_ready")
        s_wkv = sem("wkv_split")
        s_wrest = sem("ffn_weights_ready")
        s_passed = {e: sem(f"passed_{e}") for e in ("sp", "pool", "pe", "dve")}
        s_xt = sem("xt_loaded")
        s_xhi = sem("x_hi_ready")
        s_xs = sem("x_split")
        s_q1 = sem("q_part1_ready")
        s_qr = sem("q_rest_ready")
        s_q2 = sem("q_part2_ready")
        s_q3 = sem("q_part3_ready")
        s_job = sem("projection_ready")
        s_ev = sem("projection_copied")
        s_k1 = sem("k_part1_ready")
        s_kr = sem("k_rest_ready")
        s_k2 = sem("k_part2_ready")
        s_k3 = sem("k_part3_ready")
        s_qst = sem("q_stored")
        s_kst = sem("k_stored")
        s_vst = [sem(f"v_tile_stored{i}") for i in range(UT)]
        s_stack = [sem(f"stack_loaded{i}") for i in range(RING)]
        s_v = [sem(f"v_loaded{i}") for i in range(RING)]
        s_sc = sem("scores_ready")
        s_max = sem("negmax_ready")
        s_den = sem("den_ready")
        s_ln = sem("lnden_ready")
        s_shc = sem("shift_chain")
        s_shp = sem("shift_parts_ready")
        s_shs = sem("shifts_transposed")
        s_shd = sem("shift_in_dram")
        s_shl = [sem(f"shift_rows_loaded{i}") for i in range(RING)]
        s_st = sem("scoresT_ready")
        s_w = sem("weights_made")
        s_sel = sem("weights_masked")
        s_pv = sem("weights_used")
        s_oev = sem("o_copied")
        s_ost = [sem(f"o_stored{i}") for i in range(2)]
        s_g = [sem(f"g_loaded{i}") for i in range(2)]
        s_xn = [sem(f"xn_loaded{i}") for i in range(2)]
        s_gelu = sem("gelu_done")
        s_wf = sem("wf_ready")
        s_x2 = sem("x_doubled")
        s_y = sem("y_pre_ready")
        s_bs = sem("stats_ready")
        s_mv = sem("mean_var_ready")
        s_lv = sem("lnvar_ready")
        s_r0 = sem("rstd0_ready")
        s_nw = sem("newton_chain")
        s_yn = sem("y_ready")
        s_zn = sem("z_ready")
        s_yt = sem("yT_ready")
        s_yh = sem("y_hi_ready")
        s_yl = sem("y_lo_ready")
        s_gu = sem("gate_up_ready")
        s_si = sem("silu_ready")
        s_h = sem("h_ready")
        s_hh = sem("h_hi_ready")
        s_hl = sem("h_lo_ready")
        s_dn = sem("down_ready")
        s_z = sem("z_pre_ready")
        s_out = [sem(f"out_stored{i}") for i in range(2)]

        block = ctx.enter_context(nc.Block())

        JOBS = [("k", c, 0) for c in range(DC)] + [("v", i, hf) for i in range(UT) for hf in range(2)]
        NB = len(a_banks)
        NJ = len(JOBS)
        SHARE = (range(0, 3), range(3, 6), range(6, 8), range(8, 10))
        b_bank = oo[:, 0:BANK]
        ALONE = 2

        def unit_beside(r, it):
            a = r // 4 + ALONE
            return a + it if a < UNITS else None

        def jobs_beside(r, it):
            return () if unit_beside(r, it) is None else tuple(enumerate(SHARE[r % 4]))

        def weights(h, u, c0, c1):
            return W[h][u][:, c0 - P * u:c1 - P * u]

        def chunks(u):
            return [(P * u, BANK), (BANK, S)] if P * u < BANK else [(P * u, S)]

        CH = [len(chunks(u)) for u in range(NT)]
        PER_ST = 2 * sum(CH)

        def made(u, h):
            return 2 * sum(CH[:u]) + (CH[u] if h else 0)

        ORDER = (0,) + tuple(range(NT - 1, 0, -1))
        LAG = 2
        BEHIND = 3
        STEPS_B = PAIRS + LAG
        LOOP_B = (STEPS_B, 4, 4, UNITS - ALONE - 2)
        STEPS_C = UNITS + 1
        LOOP_C = (STEPS_C, 3, 2, (UNITS - 6) // 2)

        def unit_of(r, it):
            return r // 2 + it, (r % 2) * U

        @block.sync
        def _(sp):
            def load_x(a, first=False):
                if not first:
                    sp.wait_ge(s_q3, DC * a)
                    settle(sp, s_passed["sp"])
                sp.dma_start(xt[:], xT[bass.ds(a // 2, 1), :, bass.ds(a % 2 * U, U)].rearrange(
                    "o (c p) t -> (o p) c t", p=P)).then_inc(s_xt, 16)

            def store_parts(parts, split, stored, a):
                for m in range(PARTS):
                    sp.dma_start(parts[m, bass.ds(a // 2 * D, D), bass.ds(a % 2 * U, U)].rearrange(
                        "(c p) t -> p c t", p=P), split[:, m]).then_inc(stored, 16)

            def store_q(a):
                sp.wait_ge(s_q3, DC * (a + 1))
                settle(sp, s_passed["sp"])
                store_parts(qd, qp, s_qst, a)

            def store_k(a):
                sp.wait_ge(s_k3, DC * (a + 1))
                settle(sp, s_passed["sp"])
                store_parts(kd, kp, s_kst, a)

            def store_v(a, i):
                sp.wait_ge(s_ev, NJ * a + DC + 2 * (i + 1))
                settle(sp, s_passed["sp"])
                sp.dma_start(vd[bass.ds(a // 2 * HC, HC), bass.ds(a % 2 * UT + i, 1)].rearrange(
                    "h o t v -> (o t) h v"), vs[:, i].rearrange("t (h v) -> t h v", v=P)
                    ).then_inc(s_vst[i], 16)

            def load_stacks(r, it):
                n = r + RING * it
                slot = r % RING
                if r % 4 == 0:
                    for stored in (s_qst, s_kst):
                        sp.wait_ge(stored, 16 * PARTS * (min(r // 4 + 2, UNITS) + it))
                        settle(sp, s_passed["sp"])
                if r >= RING:
                    sp.wait_ge(s_w, PER_ST * (n - RING + 1))
                    settle(sp, s_passed["sp"])
                for (stack, parts, rows) in ((Q, qd, Q_ROWS), (K, kd, K_ROWS)):
                    for i, m in enumerate(rows):
                        sp.dma_start(stack[slot][DH * i:DH * (i + 1), :, :],
                                     parts[m, bass.ds(n * 2 * DH, 2 * DH), :].rearrange(
                                         "(h d) t -> d h t", d=DH)).then_inc(s_stack[slot], 16)

            def load_v(r, it):
                n = r + RING * it
                slot = r % RING
                if r % 4 == 0:
                    for stored in s_vst:
                        sp.wait_ge(stored, 16 * (min(r // 4 + 2, UNITS) + it))
                        settle(sp, s_passed["sp"])
                if r >= RING:
                    sp.wait_ge(s_pv, NT * (n - RING + 1))
                    settle(sp, s_passed["sp"])
                sp.dma_start(V[slot][:], vd[bass.ds(n, 1)].rearrange("o k t v -> (o t) k v")
                             ).then_inc(s_v[slot], 16)

            def attend(r, it):
                n = r + RING * it
                if r + 1 < PAIRS:
                    load_stacks(r + 1, it)
                a, k = unit_beside(r, it), r % 4
                if a is not None:
                    if k == 2:
                        if r // 4 + ALONE + 1 < UNITS:
                            load_x(a + 1)
                        store_k(a)
                        store_v(a, 0)
                        store_v(a, 1)
                    if k == 3:
                        store_v(a, 2)
                if 1 <= r <= PAIRS:
                    sp.wait_ge(s_shs, n)
                    settle(sp, s_passed["sp"])
                    sp.dma_start(sd[bass.ds(n - 1, 1)].rearrange("o p c -> (o p) c"),
                                 shiftT[:].rearrange("p m a -> p (m a)")).then_inc(s_shd, 16)
                    sp.wait_ge(s_shd, 16 * n)
                    settle(sp, s_passed["sp"])
                    slot = (r - 1) % RING
                    for m in range(PARTS):
                        c, row = m * 2 * NT // SQ, m * 2 * NT % SQ
                        sp.dma_start(
                            Q[slot][SPL + m:SPL + m + 1, :, :].rearrange(
                                "m h (u s q) -> m (h u) s q", s=P // SQ, q=SQ),
                            sd[bass.ds(n - 1, 1), :, SQ * c:SQ * (c + 1)].rearrange(
                                "o (s a) q -> o a s q", a=SQ)[:, row:row + 2 * NT]).then_inc(s_shl[slot], 16)
                if r >= LAG + 1:
                    sp.wait_ge(s_oev, 2 * (n - LAG))
                    settle(sp, s_passed["sp"])
                    store_o(r - LAG - 1, n - LAG - 1)
                if a is not None and k == 3:
                    store_v(a, 3)
                if r + 1 < PAIRS:
                    load_v(r + 1, it)
                if a is not None and k == 1:
                    store_q(a)
                if r == PAIRS - 1:
                    sp.wait_ge(s_job, NJ * UNITS)
                    sp.wait_ge(s_ev, NJ * UNITS)
                    sp.wait_ge(s_k3, DC * UNITS)
                    for i in range(2):
                        sp.wait_ge(s_ost[i], 16 * (PAIRS // B // 2))
                    load_unit(0, 0)
                    load_unit(1, 0)

            def store_o(r, n):
                sp.dma_start(od.rearrange("b h t -> (b h) t")[bass.ds(n * P, P), :],
                             osb[r % 2][:]).then_inc(s_ost[r % 2], 16)

            def load_unit(r, it):
                b, t0 = unit_of(r, it)
                n = r + 2 * it
                if r >= 2:
                    sp.wait_ge(s_wf, UT * (n - 1))
                    settle(sp, s_passed["sp"])
                    sp.wait_ge(s_y, UT * (n - 1))
                    settle(sp, s_passed["sp"])
                sp.dma_start(g[r % 2][:], od[bass.ds(b, 1), :, t0:t0 + U].rearrange(
                    "o (c p) t -> (o p) c t", p=P)).then_inc(s_g[r % 2], 16)
                sp.dma_start(xn[r % 2][:], x[bass.ds(n * U, U), :].rearrange(
                    "(i p) d -> p i d", p=P)).then_inc(s_xn[r % 2], 16)

            load_x(0, True)
            sp.dma_start(wk_in[:], Wk.rearrange("(c p) n -> p c n", p=P)).then_inc(s_wk_in, 16)
            sp.dma_start(wv_in[:], Wv.rearrange("(c p) n -> p c n", p=P)).then_inc(s_wv_in, 16)
            sp.dma_start(bk_sb[:], bk).then_inc(s_bk, 16)
            sp.dma_start(bv_sb[:], bv).then_inc(s_w_in, 16)
            sp.dma_start(bf_sb[:], bf.partition_broadcast(P)).then_inc(s_w_in, 16)
            sp.dma_start(wf_sb[:], Wf.rearrange("(c p) n -> p c n", p=P)).then_inc(s_w_in, 16)
            sp.dma_start(wi_in[0][:].rearrange("p (c n) -> p c n", c=DC),
                         wg.rearrange("(c p) n -> p c n", p=P)).then_inc(s_w_in, 16)
            sp.dma_start(wi_in[1][:].rearrange("p (c n) -> p c n", c=DC),
                         wu.rearrange("(c p) n -> p c n", p=P)).then_inc(s_w_in, 16)
            sp.dma_start(wi_in[2][:].rearrange("p (c n) -> p c n", c=FC),
                         wd.rearrange("(c p) n -> p c n", p=P)).then_inc(s_w_in, 16)
            for a in range(ALONE):
                store_q(a)
                load_x(a + 1)
                store_k(a)
                if a == 1:
                    load_stacks(0, 0)
                for i in range(UT):
                    store_v(a, i)
            load_v(0, 0)
            walk(sp, *LOOP_B, attend)
            sp.wait_ge(s_oev, 2 * PAIRS)
            store_o(PAIRS - 1, PAIRS - 1)
            for i in range(2):
                sp.wait_ge(s_ost[i], 16 * PAIRS // 2)

            def finish(r, it):
                n = r + 2 * it
                if r + 2 < UNITS:
                    load_unit(r + 2, it)
                if r >= 1:
                    sp.wait_ge(s_zn, UT * n)
                    settle(sp, s_passed["sp"])
                    sp.dma_start(out[bass.ds((n - 1) * U, U), :].rearrange("(i p) d -> p i d", p=P),
                                 z[(r - 1) % 2][:]).then_inc(s_out[(r - 1) % 2], 16)

            walk(sp, *LOOP_C, finish)
            for i in range(2):
                sp.wait_ge(s_out[i], 16 * UNITS // 2)

        @block.gpsimd
        def _(pool):
            pool.memset(ident16[:], 0.0).then_inc(s_blank, 1)
            pool.memset(ident32[:], 0.0).then_inc(s_blank, 1)
            pool.memset(causal[:], 0.0).then_inc(s_blank, 1)
            pool.wait_ge(s_blank, 3)
            for m in (ident16, ident32):
                pool.affine_select(out=m[:], in_=m[:], compare_op=ALU.not_equal, fill=1.0, base=0,
                                   pattern=[[-1, P]], channel_multiplier=1).then_inc(s_const, 1)
            pool.affine_select(out=causal[:], in_=causal[:], compare_op=ALU.is_ge, fill=MASKED, base=0,
                               pattern=[[-1, P]], channel_multiplier=1).then_inc(s_const, 1)

            def q_rest(a, c):
                pool.wait_ge(s_xs, a + 1)
                pool.wait_ge(s_q1, DC * a + c + 1)
                pool.tensor_tensor(xt[:, c], xt[:, c], qp[:, 0, c], ALU.subtract).then_inc(s_qr, 1)

            def q_part3(a, c):
                pool.wait_ge(s_q2, DC * a + c + 1)
                pool.tensor_tensor(qp[:, 2, c], xt[:, c], qp[:, 1, c], ALU.subtract).then_inc(s_q3, 1)

            def k_rest(a, c):
                pool.wait_ge(s_k1, DC * a + c + 1)
                pool.tensor_tensor(kf[:, c], kf[:, c], kp[:, 0, c], ALU.subtract).then_inc(s_kr, 1)

            def k_part3(a, c):
                pool.wait_ge(s_k2, DC * a + c + 1)
                pool.tensor_tensor(kp[:, 2, c], kf[:, c], kp[:, 1, c], ALU.subtract).then_inc(s_k3, 1)

            for a in range(ALONE):
                for c in range(DC):
                    q_rest(a, c)
                    q_part3(a, c)
                for c in range(DC):
                    k_rest(a, c)
                    k_part3(a, c)

            def attend(r, it):
                n = r - LAG + RING * it
                a, k = unit_beside(r, it), r % 4
                for u in range(NT):
                    if r >= LAG:
                        for h in range(2):
                            pool.wait_ge(s_w, PER_ST * n + made(u, h) + 1)
                            settle(pool, s_passed["pool"])
                            diag = weights(h, u, P * u, P * (u + 1))
                            pool.affine_select(out=diag, in_=diag, compare_op=ALU.is_ge, fill=0.0, base=0,
                                               pattern=[[1, P]], channel_multiplier=-1).then_inc(s_sel, 1)
                    if a is not None:
                        if k == 0 and u in (6, 7):
                            q_rest(a, u - 6)
                        if k == 1 and u in (1, 2):
                            k_rest(a, u - 1)
                        if k == 1 and u in (5, 6):
                            q_part3(a, u - 5)
                        if k == 1 and u == 7:
                            for c in range(DC):
                                k_part3(a, c)

            walk(pool, *LOOP_B, attend)

            def finish(r, it):
                if r >= 1:
                    m = r - 1 + 2 * it
                    for f in range(FC):
                        pool.wait_ge(s_hh, FC * m + f + 1)
                        pool.tensor_tensor(h_lo[:, f], h32[f % 2][:], h_hi[:, f],
                                           ALU.subtract).then_inc(s_hl, 1)

            walk(pool, *LOOP_C, finish)

        @block.tensor
        def _(pe):
            def mm(o, l, r, start, stop):
                return nc.tensor.matmul(o, l, r, start=start, stop=stop)

            def job(j, a, bank):
                what, i, hf = JOBS[j]
                last = 3 * DC - 1
                for c in range(DC):
                    if what == "k":
                        cols = slice(P * i, P * (i + 1))
                        terms = ((wk_hi[:, c, cols], x_hi[:, c]), (wk_hi[:, c, cols], x_lo[:, c]),
                                 (wk_lo[:, c, cols], x_hi[:, c]))
                    else:
                        toks, cols = slice(P * i, P * (i + 1)), slice(BANK * hf, BANK * (hf + 1))
                        terms = ((x_hi[:, c, toks], wv_hi[:, c, cols]), (x_hi[:, c, toks], wv_lo[:, c, cols]),
                                 (x_lo[:, c, toks], wv_hi[:, c, cols]))
                    for k, (l, m) in enumerate(terms):
                        e = mm(bank, l, m, 3 * c + k == 0, 3 * c + k == last)
                e.then_inc(s_job, 1)

            for a in range(ALONE):
                pe.wait_ge(s_xs, a + 1)
                for j in range(NJ):
                    if a == 0 and j in (0, DC):
                        pe.wait_ge(s_wkv, 1 + j // DC)
                    if NJ * a + j >= NB:
                        pe.wait_ge(s_ev, NJ * a + j - NB + 1)
                    job(j, a, a_banks[(NJ * a + j) % NB])
            pe.wait_ge(s_ev, NJ * ALONE)
            pe.wait_ge(s_const, 3 + RING + 2)

            def job_beside(r, it, i):
                for place, j in jobs_beside(r, it):
                    if place == i:
                        a = unit_beside(r, it)
                        if j == 0:
                            pe.wait_ge(s_xs, a + 1)
                        if i == 0 and r >= LAG + 1:
                            pe.wait_ge(s_oev, 2 * (r - LAG - 1 + RING * it) + 1)
                        if i > 0:
                            pe.wait_ge(s_ev, NJ * a + j)
                        job(j, a, b_bank)

            def score(h, place, r, n):
                q, k = Q[r % RING], K[r % RING]
                u = ORDER[place]
                if place > 0 or r > 0:
                    pe.wait_ge(s_den, 2 * NT * n + 2 * place + h - 1)
                width = P * (u + 1)
                for c0 in range(0, width, BANK):
                    c1 = min(width, c0 + BANK)
                    mm(sc[h][:, c0:c1], q[0:SPL, h, P * u:P * (u + 1)], k[0:SPL, h, c0:c1], True, c1 < width)
                mm(sc[h][:, width - P:width], ident16[:], causal[:], False, True).then_inc(s_sc, 1)

            def scoreT(h, u, r, n):
                q, k = Q[r % RING], K[r % RING]
                for i, (c0, c1) in enumerate(chunks(u)):
                    c = made(u, h) + i
                    if r > 0 or c >= 2:
                        pe.wait_ge(s_w, PER_ST * n + c - 1)
                    mm(st[c % 2][:, 0:c1 - c0], k[:, h, P * u:P * (u + 1)], q[:, h, c0:c1],
                       True, True).then_inc(s_st, 1)

            def weigh(u, r, it, turn):
                n = r + RING * it
                chunk = CH[u] - 1 - turn
                if turn == 0:
                    if u == 0:
                        pe.wait_ge(s_v[r % RING], 16 * (r // RING + it + 1))
                    pe.wait_ge(s_w, PER_ST * n + made(u + 1, 0))
                    pe.wait_ge(s_sel, 2 * NT * n + 2 * (u + 1))
                if u == 0 and r > 0 and turn == 0:
                    pe.wait_ge(s_oev, 2 * n)
                if u == 0 and turn == 1:
                    jobs_copied(r, it)
                c0, c1 = chunks(u)[chunk]
                for h in range(2):
                    e = mm(oo[DV * h:DV * (h + 1), c0:c1], V[r % RING][:, u, DV * h:DV * (h + 1)],
                           weights(h, u, c0, c1), u == 0, P * (u + 1) == c1)
                if chunk == 0:
                    e.then_inc(s_pv, 1)

            def jobs_copied(r, it):
                a, share = unit_beside(r + LAG, it), SHARE[(r + LAG) % 4]
                if a is not None:
                    pe.wait_ge(s_ev, NJ * a + share[-1] + 1)

            def weigh_behind(u, r, it, turn):
                u, pair = (u - BEHIND, r - LAG) if u >= BEHIND else (u - BEHIND + NT, r - LAG - 1)
                if 0 <= pair < PAIRS and turn < CH[u]:
                    weigh(u, pair, it, turn)

            def open_pair(r, it):
                pe.wait_ge(s_stack[r % RING], 16 * (len(Q_ROWS) + len(K_ROWS)) * (r // RING + it + 1))

            def attend(r, it):
                n = r + RING * it
                weighing = r >= LAG
                m, rm = n - LAG, r - LAG
                for u in range(NT):
                    def next_score(h):
                        if u + 1 < NT and r < PAIRS:
                            score(h, u + 1, r, n)
                        elif u + 1 == NT and r + 1 < PAIRS:
                            if h == 0:
                                open_pair(r + 1, it)
                            score(h, 0, r + 1, n + 1)

                    next_score(0)
                    if weighing:
                        scoreT(1, u, rm, m)
                    weigh_behind(u, r, it, 0)
                    next_score(1)
                    if u + 1 < NT and weighing:
                        scoreT(0, u + 1, rm, m)
                    if u + 1 == NT and LAG <= r + 1 < STEPS_B:
                        pe.wait_ge(s_shl[(rm + 1) % RING], 16 * PARTS * ((rm + 1) // RING + it + 1))
                        scoreT(0, 0, rm + 1, m + 1)
                    weigh_behind(u, r, it, 1)
                    job_beside(r, it, u)

            open_pair(0, 0)
            score(0, 0, 0, 0)
            score(1, 0, 0, 0)
            walk(pe, *LOOP_B, attend)
            for u in range(BEHIND):
                weigh_behind(u, STEPS_B, 0, 0)
            pe.wait_ge(s_oev, 2 * PAIRS)
            pe.wait_ge(s_wrest, 3)

            wf_ps, yt_ps, dn_ps = sc[0], sc[1], sc[1]
            gate_ps = [st[0][:, :], oo[:, 0:BANK]]
            up_ps = [st[1][:, :], oo[:, BANK:]]

            def wf_product(r, n, tiles):
                for i in tiles:
                    if i == 0 and r > 0:
                        pe.wait_ge(s_y, UT * n)
                    for c in range(HC):
                        if i == 0:
                            pe.wait_ge(s_gelu, HC * n + c + 1)
                        e = mm(wf_ps[:, D * i:D * (i + 1)], g[r % 2][:, c, P * i:P * (i + 1)], wf_sb[:, c],
                               c == 0, c == HC - 1)
                    e.then_inc(s_wf, 1)

            def transpose_y(r, m):
                if r > 0:
                    pe.wait_ge(s_z, UT * m)
                for i in range(UT):
                    pe.wait_ge(s_yn, UT * m + i + 1)
                    for c in range(DC):
                        e = nc.tensor.transpose(yt_ps[:, BANK * c + P * i:BANK * c + P * (i + 1)],
                                                y[r % 2][:, i, P * c:P * (c + 1)], ident32[:])
                e.then_inc(s_yt, 1)

            def gate_up(r, m):
                pe.wait_ge(s_yl, DC * (m + 1))
                for f in range(FC):
                    if r > 0 or f >= 2:
                        pe.wait_ge(s_h, FC * m + f - 1)
                    cols = slice(P * f, P * (f + 1))
                    for ps, w in ((gate_ps[f % 2], wg_sb), (up_ps[f % 2], wu_sb)):
                        for c in range(DC):
                            for k, part in enumerate((y_hi, y_lo)):
                                e = mm(ps, w[:, c, cols], part[:, c], c + k == 0, c == DC - 1 and k == 1)
                    e.then_inc(s_gu, 1)

            def down(m):
                for i in range(UT):
                    for f in range(FC):
                        if i == 0:
                            pe.wait_ge(s_hl, FC * m + f + 1)
                        for k, part in enumerate((h_hi, h_lo)):
                            e = mm(dn_ps[:, D * i:D * (i + 1)], part[:, f, P * i:P * (i + 1)], wd_sb[:, f],
                                   f + k == 0, f == FC - 1 and k == 1)
                    e.then_inc(s_dn, 1)

            def finish(r, it):
                n = r + 2 * it
                if r < UNITS:
                    wf_product(r, n, (0, 1))
                if r >= 1:
                    transpose_y(r - 1, n - 1)
                if r < UNITS:
                    wf_product(r, n, (2,))
                if r >= 1:
                    gate_up(r - 1, n - 1)
                if r < UNITS:
                    wf_product(r, n, (3,))
                if r >= 1:
                    down(n - 1)

            walk(pe, *LOOP_C, finish)

        @block.scalar
        def _(act):
            def copy(o, i):
                return nc.scalar.activation(o, i, ACT.Copy)

            act.preload_act_table_set(LN_EXP)
            act.wait_ge(s_wkv, 2)
            act.wait_ge(s_wrest, 3)
            act.wait_ge(s_const, 3 + RING + 2)

            def attend(r, it):
                n = r + RING * it
                if 1 <= r <= PAIRS:
                    act.wait_ge(s_den, 2 * NT * n)
                    if r >= 2:
                        act.wait_ge(s_shp, n - 1)
                    nc.scalar.activation(lnden[:], den[(r - 1) % 2][:], ACT.Ln).then_inc(s_ln, 1)
                if r >= 2 and r < PAIRS:
                    act.wait_ge(s_shp, n - 1)
                for u in range(NT):
                    for h in range(2):
                        if r < PAIRS:
                            a = 2 * u + h
                            act.wait_ge(s_max, 2 * NT * n + a + 1)
                            width = P * (ORDER[u] + 1)
                            slot = slice(NT * h + ORDER[u], NT * h + ORDER[u] + 1)
                            nc.scalar.activation(scrap[h][:, 0:width], sc[h][:, 0:width], ACT.Exp,
                                                 bias=negmax[r % 2][:, slot], accum_out=den[r % 2][:, slot]
                                                 ).then_inc(s_den, 1)
                        if r >= LAG:
                            m, rm = n - LAG, r - LAG
                            for i, (c0, c1) in enumerate(chunks(u)):
                                c = made(u, h) + i
                                act.wait_ge(s_st, PER_ST * m + c + 1)
                                if i == 0 and rm > 0:
                                    act.wait_ge(s_pv, NT * (m - 1) + u + 1)
                                nc.scalar.activation(weights(h, u, c0, c1), st[c % 2][:, 0:c1 - c0],
                                                     ACT.Exp).then_inc(s_w, 1)

            walk(act, *LOOP_B, attend)

            def gelus(r, n, stored):
                act.wait_ge(s_g[r % 2], 16 * (stored + 1))
                for c in range(HC):
                    nc.scalar.activation(g[r % 2][:, c], g[r % 2][:, c], ACT.Gelu,
                                         bias=bv_sb[:, c:c + 1]).then_inc(s_gelu, 1)

            gate_ps = [st[0][:, :], oo[:, 0:BANK]]
            gelus(0, 0, 0)

            def finish(r, it):
                n = r + 2 * it
                if r >= 1:
                    m = n - 1
                    act.wait_ge(s_yt, m + 1)
                    for c in range(DC):
                        copy(y_hi[:, c], sc[1][:, BANK * c:BANK * (c + 1)]).then_inc(s_yh, 1)
                    for f in range(FC + 1):
                        if f < FC:
                            act.wait_ge(s_gu, FC * m + f + 1)
                            nc.scalar.activation(sg[f % 2][:], gate_ps[f % 2], ACT.Silu,
                                                 scale=QSCALE).then_inc(s_si, 1)
                        if f > 0:
                            if f == 1 and r >= 2:
                                act.wait_ge(s_dn, UT * m)
                            act.wait_ge(s_h, FC * m + f)
                            copy(h_hi[:, f - 1], h32[(f - 1) % 2][:]).then_inc(s_hh, 1)
                if r + 1 < UNITS:
                    gelus(r + 1, n + 1, (r + 1) // 2 + it)
                a0, a1 = (0 if r < UNITS else UT), (2 * UT if r >= 1 else UT)
                act.preload_act_table_set(LN_EXP)
                act.wait_ge(s_mv, n + 1)
                nc.scalar.activation(lnvar[:, a0:a1], mv[:, a0:a1, 1], ACT.Ln, bias=eps_sb[:]).then_inc(s_lv, 1)
                act.wait_ge(s_lv, n + 1)
                nc.scalar.activation(rstd0[:, a0:a1], lnvar[:, a0:a1], ACT.Exp, scale=-0.5).then_inc(s_r0, 1)

            walk(act, *LOOP_C, finish)

        @block.vector
        def _(dve):
            v = nc.vector
            for i in range(RING):
                v.memset(K[i][SPL:ROWS, :, :], 1.0).then_inc(s_const, 1)
            v.memset(eps_sb[:], EPS).then_inc(s_const, 1)
            v.memset(shift_parts[:], 0.0).then_inc(s_const, 1)

            def split_weights(k, hi, lo, landed, loaded):
                dve.wait_ge(loaded, 16)
                v.tensor_copy(hi[:], landed[:]).then_inc(s_w_hi, 1)
                dve.wait_ge(s_w_hi, k + 1)
                v.tensor_tensor(lo[:], landed[:], hi[:].bitcast(F32), ALU.subtract).then_inc(s_wkv, 1)

            def ffn_weights():
                dve.wait_ge(s_w_in, 16 * 6)
                for dst, src in ((wg_sb, wi_in[0]), (wu_sb, wi_in[1]), (wd_sb, wi_in[2])):
                    v.tensor_copy(dst[:].rearrange("p c n -> p (c n)"), src[:]).then_inc(s_wrest, 1)

            def x_part1(a, first=False):
                dve.wait_ge(s_xt, 16 * (a + 1))
                if not first:
                    dve.wait_ge(s_job, NJ * a)
                v.tensor_copy(x_hi[:], xt[:]).then_inc(s_xhi, 1)

            def x_part2(a):
                dve.wait_ge(s_xhi, a + 1)
                v.tensor_tensor(x_lo[:], xt[:], x_hi[:].bitcast(F32), ALU.subtract).then_inc(s_xs, 1)

            def q_part1(a, c, first=False):
                if not first:
                    dve.wait_ge(s_qst, 16 * PARTS * a)
                v.tensor_copy(qp[:, 0, c], xt[:, c]).then_inc(s_q1, 1)

            def q_part2(a, c):
                dve.wait_ge(s_qr, DC * a + c + 1)
                v.tensor_copy(qp[:, 1, c], xt[:, c]).then_inc(s_q2, 1)

            def k_part1(a, c, first=False):
                dve.wait_ge(s_ev, NJ * a + c + 1)
                if not first:
                    dve.wait_ge(s_kst, 16 * PARTS * a)
                v.tensor_copy(kp[:, 0, c], kf[:, c]).then_inc(s_k1, 1)

            def k_part2(a, c):
                dve.wait_ge(s_kr, DC * a + c + 1)
                v.tensor_copy(kp[:, 1, c], kf[:, c]).then_inc(s_k2, 1)

            def copy_out(j, a, bank, first=False):
                what, i, hf = JOBS[j]
                dve.wait_ge(s_job, NJ * a + j + 1)
                if what == "k":
                    if not first:
                        dve.wait_ge(s_k3, DC * (a - 1) + i + 1)
                    v.tensor_scalar(kf[:, i], bank, bk_sb[:, i:i + 1], None, ALU.add).then_inc(s_ev, 1)
                else:
                    if not first and hf == 0:
                        dve.wait_ge(s_vst[i], 16 * a)
                    v.tensor_copy(vs[:, i, BANK * hf:BANK * (hf + 1)], bank).then_inc(s_ev, 1)

            x_part1(0, True)
            x_part2(0)
            split_weights(0, wk_hi, wk_lo, wk_in, s_wk_in)
            split_weights(1, wv_hi, wv_lo, wv_in, s_wv_in)
            dve.wait_ge(s_bk, 16)
            for c in range(DC):
                q_part1(0, c, True)
            for a in range(ALONE):
                for j in range(NJ):
                    copy_out(j, a, a_banks[(NJ * a + j) % NB], a == 0)
                    if j < DC:
                        k_part1(a, j, a == 0)
                    if j in (2, 3):
                        q_part2(a, j - 2)
                    if j in (4, 5):
                        k_part2(a, j - 4)
                x_part1(a + 1)
                x_part2(a + 1)
                if a + 1 < ALONE:
                    for c in range(DC):
                        q_part1(a + 1, c)
            ffn_weights()

            def shifts(r, n, step):
                if step == 0:
                    dve.wait_ge(s_ln, n)
                elif step < 5:
                    dve.wait_ge(s_shc, 4 * (n - 1) + step)
                if step == 0:
                    v.tensor_tensor(shift[:], negmax[(r - 1) % 2][:], lnden[:], ALU.subtract).then_inc(s_shc, 1)
                if step == 1:
                    if r >= 2:
                        dve.wait_ge(s_shs, n - 1)
                    v.tensor_copy(shift_parts[:, 0], shift[:]).then_inc(s_shc, 1)
                if step == 2:
                    v.tensor_tensor(shift_r1[:], shift[:], shift_parts[:, 0], ALU.subtract).then_inc(s_shc, 1)
                if step == 3:
                    v.tensor_copy(shift_parts[:, 1], shift_r1[:]).then_inc(s_shc, 1)
                if step == 4:
                    v.tensor_tensor(shift_parts[:, 2], shift_r1[:], shift_parts[:, 1],
                                    ALU.subtract).then_inc(s_shp, 1)
                if step == 5:
                    dve.wait_ge(s_shp, n)
                    if r >= 2:
                        dve.wait_ge(s_shd, 16 * (n - 1))
                    settle(dve, s_passed["dve"])
                    v.transpose(shiftT[:].rearrange("p m a -> p (m a)"),
                                shift_parts[:].rearrange("p m a -> p (m a)")).then_inc(s_shs, 1)

            def attend(r, it):
                n = r + RING * it
                a, k = unit_beside(r, it), r % 4
                for u in range(NT):
                    for h in range(2):
                        if r < PAIRS:
                            dve.wait_ge(s_sc, 2 * NT * n + 2 * u + h + 1)
                            slot = NT * h + ORDER[u]
                            v.tensor_reduce(negmax[r % 2][:, slot:slot + 1], sc[h][:, 0:P * (ORDER[u] + 1)],
                                            AX.X, ALU.max, negate=True).then_inc(s_max, 1)
                        if 2 * u + h < 6 and 1 <= r <= PAIRS:
                            shifts(r, n, 2 * u + h)
                        if h == 0 and u == 0 and r >= LAG + 1:
                            copy_o(0, r - LAG - 1, n - LAG - 1, it)
                        if h == 0 and u == BEHIND and r >= LAG + 1:
                            copy_o(1, r - LAG - 1, n - LAG - 1, it)
                    for i, j in jobs_beside(r, it):
                        if i + 1 == u:
                            copy_out(j, a, b_bank)
                    if a is not None:
                        if k == 0 and u in (4, 7):
                            k_part1(a, (u - 4) // 3)
                        if k == 0 and u in (5, 6):
                            q_part1(a, u - 5)
                        if k == 1 and u in (4, 5):
                            q_part2(a, u - 4)
                        if k == 1 and u in (6, 7):
                            k_part2(a, u - 6)
                        if k == 3 and u in (3, 5) and r // 4 + ALONE + 1 < UNITS:
                            (x_part1 if u == 3 else x_part2)(a + 1)

            def copy_o(half, r, n, it):
                dve.wait_ge(s_pv, NT * n + (NT if half else NT // 2))
                if half == 0 and r >= 2:
                    dve.wait_ge(s_ost[r % 2], 16 * (r // 2 + (RING // 2) * it))
                cols = slice(BANK * half, BANK * (half + 1))
                v.tensor_copy(osb[r % 2][:, cols], oo[:, cols]).then_inc(s_oev, 1)

            walk(dve, *LOOP_B, attend)
            for half in range(2):
                copy_o(half, PAIRS - 1, PAIRS - 1, 0)
            for i in range(2):
                dve.wait_ge(s_ost[i], 16 * PAIRS // 2)

            wf_ps, yt_ps, dn_ps = sc[0], sc[1], sc[1]
            up_ps = [st[1][:, :], oo[:, BANK:]]

            def statistics(i, src, made_, count):
                dve.wait_ge(made_, count)
                return v.bn_stats(stats[:, i], src)

            def finish(r, it):
                n = r + 2 * it
                w, f0 = r < UNITS, r >= 1
                def add_x(tiles):
                    for i in tiles:
                        dve.wait_ge(s_wf, UT * n + (i | 1) + 1)
                        v.tensor_tensor(y_pre[:, i], wf_ps[:, D * i:D * (i + 1)], xn[r % 2][:, i],
                                        ALU.add).then_inc(s_y, 1)

                if f0:
                    m = n - 1
                    for c in range(DC):
                        dve.wait_ge(s_yh, DC * m + c + 1)
                        v.tensor_tensor(y_lo[:, c], yt_ps[:, BANK * c:BANK * (c + 1)],
                                        y_hi[:, c].bitcast(F32), ALU.subtract).then_inc(s_yl, 1)
                if w:
                    dve.wait_ge(s_xn[r % 2], 16 * (r // 2 + it + 1))
                    v.scalar_tensor_tensor(xn[r % 2][:], xn[r % 2][:], 2.0,
                                           bf_sb[:].unsqueeze(1).to_broadcast([P, UT, D]),
                                           ALU.mult, ALU.add).then_inc(s_x2, 1)
                    dve.wait_ge(s_x2, n + 1)
                    if r > 0:
                        dve.wait_ge(s_yn, UT * n)
                    add_x((0, 1))
                if f0:
                    if r >= 2:
                        dve.wait_ge(s_zn, UT * m)
                    for f in range(FC):
                        dve.wait_ge(s_si, FC * m + f + 1)
                        if r >= 2 or f >= 2:
                            dve.wait_ge(s_hl, FC * m + f - 1)
                        v.scalar_tensor_tensor(h32[f % 2][:], up_ps[f % 2], QSCALE * HSCALE, sg[f % 2][:],
                                               ALU.mult, ALU.mult).then_inc(s_h, 1)
                if w:
                    add_x((2, 3))
                if w:
                    for i in range(UT):
                        statistics(i, y_pre[:, i], s_y, UT * n + i + 1).then_inc(s_bs, 1)
                if f0:
                    for i in range(UT):
                        dve.wait_ge(s_dn, UT * m + (i | 1) + 1)
                        v.scalar_tensor_tensor(z_pre[:, i], dn_ps[:, D * i:D * (i + 1)], QSCALE / HSCALE,
                                               y[(r - 1) % 2][:, i], ALU.mult, ALU.add).then_inc(s_z, 1)
                if f0:
                    for i in range(UT):
                        statistics(UT + i, z_pre[:, i], s_z, UT * (n - 1) + i + 1).then_inc(s_bs, 1)
                a0, a1 = (0 if w else UT), (2 * UT if f0 else UT)
                done = 2 * UT * n - (UT if r >= 1 else 0)
                dve.wait_ge(s_bs, done + a1 - a0)
                settle(dve, s_passed["dve"])
                for a in range(a0, a1):
                    e = v.bn_aggr(mv[:, a], stats[:, a])
                e.then_inc(s_mv, 1)
                dve.wait_ge(s_r0, n + 1)
                sl = slice(a0, a1)
                v.scalar_tensor_tensor(newt[:, 0, sl], mv[:, sl, 1], EPS, rstd0[:, sl],
                                       ALU.add, ALU.mult).then_inc(s_nw, 1)
                dve.wait_ge(s_nw, 4 * n + 1)
                v.tensor_tensor(newt[:, 1, sl], newt[:, 0, sl], rstd0[:, sl], ALU.mult).then_inc(s_nw, 1)
                dve.wait_ge(s_nw, 4 * n + 2)
                v.tensor_scalar(newt[:, 2, sl], newt[:, 1, sl], -0.5, 1.5, ALU.mult, ALU.add).then_inc(s_nw, 1)
                dve.wait_ge(s_nw, 4 * n + 3)
                v.tensor_tensor(rstd[:, sl], newt[:, 2, sl], rstd0[:, sl], ALU.mult).then_inc(s_nw, 1)
                dve.wait_ge(s_nw, 4 * n + 4)
                if w:
                    for i in range(UT):
                        v.tensor_scalar(y[r % 2][:, i], y_pre[:, i], mv[:, i, 0:1], rstd[:, i:i + 1],
                                        ALU.subtract, ALU.mult).then_inc(s_yn, 1)
                if f0:
                    if r >= 3:
                        dve.wait_ge(s_out[(r - 1) % 2], 16 * ((r - 1) // 2 + it))
                    for i in range(UT):
                        a = UT + i
                        v.tensor_scalar(z[(r - 1) % 2][:, i], z_pre[:, i], mv[:, a, 0:1], rstd[:, a:a + 1],
                                        ALU.subtract, ALU.mult).then_inc(s_zn, 1)

            walk(dve, *LOOP_C, finish)


def kernel(**inputs):
    import concourse.bacc as bacc
    import numpy as np
    from concourse.bass_utils import run_bass_kernel_spmd

    a = {k.removeprefix("L0_"): np.asarray(v) for k, v in inputs.items()}
    x = a["attn_x"]
    arrays = {
        "xT": np.ascontiguousarray(x.transpose(0, 2, 1)),
        "x": np.ascontiguousarray(x.reshape(-1, x.shape[-1])),
        "Wk": a["attn_Wk"], "bk": np.ascontiguousarray(a["attn_bk"].reshape(-1, P).T),
        "Wv": a["attn_Wv"], "bv": np.ascontiguousarray(a["attn_bv"].reshape(-1, P).T),
        "Wf": a["attn_Wf"], "bf": a["attn_bf"],
        "wg": np.ascontiguousarray(a["ffn_w_gate"].T), "wu": np.ascontiguousarray(a["ffn_w_up"].T),
        "wd": np.ascontiguousarray(a["ffn_w_down"].T),
    }
    nc = bacc.Bacc("TRN2", target_bir_lowering=False, num_devices=1)
    args = [nc.dram_tensor(f"in_{n}", v.shape, mybir.dt.from_np(v.dtype), kind="ExternalInput").ap()
            for n, v in arrays.items()]
    out = nc.dram_tensor("out", (x.shape[0] * x.shape[1], x.shape[2]), F32, kind="ExternalOutput").ap()
    build(nc, *args, out)
    r = run_bass_kernel_spmd(nc, [{f"in_{n}": v for n, v in arrays.items()}], core_ids=[0])
    return r.results[0]["out"].reshape(x.shape)
```
